# Optimizing a Trainium2 kernel written in Bass

```python
import numpy as np
import jax
import jax.numpy as jnp

def _softmax(x, axis=-1):
    return jax.nn.softmax(x, axis=axis)

def _gelu(x):
    return jax.nn.gelu(x, approximate=True)

def _silu(x):
    return jax.nn.silu(x)

def _sigmoid(x):
    return jax.nn.sigmoid(x)

def _layernorm(x, axis=-1, eps=1e-05):
    m = jnp.mean(x, axis=axis, keepdims=True)
    v = jnp.var(x, axis=axis, keepdims=True)
    return (x - m) / jnp.sqrt(v + eps)

def _scatter_add(tgt, idx, src, axis=0):
    return tgt.at[idx].add(src)

def _segment_sum(src, seg, n):
    return jax.ops.segment_sum(src, seg, n)
kernel_name = 'mk_gnn_ffn_d2_gnn_r32_c229bf'

def setup_inputs(seed: int=0):
    np.random.seed(seed)
    _w = jnp.asarray

    def _rec_inputs():
        import jax
        import jax.numpy as jnp
        _gk = jax.random.key(seed)
        x = -0.0002117 + 1 * jax.random.normal(jax.random.fold_in(_gk, 1), (3125, 256), jnp.float32)
        _s = jax.random.randint(jax.random.fold_in(_gk, 2), (25000,), 0, 3125, jnp.int32)
        _d = jax.random.randint(jax.random.fold_in(_gk, 3), (25000,), 0, 3125, jnp.int32)
        _loop = jnp.arange(3125, dtype=jnp.int32)
        src = jnp.concatenate([_s, _d, _loop])
        dst = jnp.concatenate([_d, _s, _loop])
        _o = jnp.argsort(dst, stable=True)
        src = src[_o]
        dst = dst[_o]
        edge_weight = jax.random.uniform(jax.random.fold_in(_gk, 13), (53125,), jnp.float32, 0.0, 1)
        return (x, src, dst, edge_weight)
    x, src, dst, edge_weight = _rec_inputs()

    def _L0_gnn_setup():
        import jax, jax.numpy as jnp
        import numpy as np
        N_NODES = 3125
        N_EDGES = 100000
        D_IN = 256
        D_OUT = 256
        key = jax.random.key(seed)
        k1, k2, k3, k4, k5, k6 = jax.random.split(key, 6)
        x = jax.random.normal(k1, (N_NODES, D_IN), dtype=jnp.float32)
        edge_row = jax.random.randint(k2, (N_EDGES,), 0, N_NODES, dtype=jnp.int32)
        edge_col = jax.random.randint(k3, (N_EDGES,), 0, N_NODES, dtype=jnp.int32)
        edge_val = jax.random.uniform(k4, (N_EDGES,), dtype=jnp.float32)
        bound = 1.0 / np.sqrt(D_IN)
        W = jax.random.uniform(k5, (D_OUT, D_IN), minval=-bound, maxval=bound, dtype=jnp.float32)
        b = jax.random.uniform(k6, (D_OUT,), minval=-bound, maxval=bound, dtype=jnp.float32)
        return {'x': x, 'edge_row': edge_row, 'edge_col': edge_col, 'edge_val': edge_val, 'W': W, 'b': b}
    _L0_gnn_all = _L0_gnn_setup()
    _L0_gnn_in = {k: v for k, v in _L0_gnn_all.items() if k in ('W', 'b')}
    del _L0_gnn_all

    def _L0_ffn_setup():
        import jax, jax.numpy as jnp
        import numpy as np
        B, S, D, H, E, K = (8, 256, 256, 1024, 8, 2)
        key = jax.random.key(seed)
        ks = jax.random.split(key, 7)
        s_in = 1.0 / np.sqrt(D)
        s_hid = 1.0 / np.sqrt(H)
        return {'x': jax.random.normal(ks[0], (B, S, D), dtype=jnp.float32), 'Wg': jax.random.uniform(ks[1], (E, D), jnp.float32, -s_in, s_in), 'bg': jax.random.uniform(ks[2], (E,), jnp.float32, -s_in, s_in), 'W1': jax.random.uniform(ks[3], (E, H, D), jnp.float32, -s_in, s_in), 'b1': jax.random.uniform(ks[4], (E, H), jnp.float32, -s_in, s_in), 'W2': jax.random.uniform(ks[5], (E, D, H), jnp.float32, -s_hid, s_hid), 'b2': jax.random.uniform(ks[6], (E, D), jnp.float32, -s_hid, s_hid)}
    _L0_ffn_all = _L0_ffn_setup()
    _L0_ffn_in = {k: v for k, v in _L0_ffn_all.items() if k in ('Wg', 'bg', 'W1', 'b1', 'W2', 'b2')}
    del _L0_ffn_all

    def _L1_gnn_setup():
        import jax, jax.numpy as jnp
        import numpy as np
        N_NODES = 3125

        def sage_conv(x, edge_index, Wl, bl, Wr):
            src, dst = (edge_index[0], edge_index[1])
            msg = x[src]
            agg = jax.ops.segment_sum(msg, dst, num_segments=N_NODES)
            cnt = jax.ops.segment_sum(jnp.ones((edge_index.shape[1],), x.dtype), dst, num_segments=N_NODES)
            agg = agg / jnp.maximum(cnt, 1.0)[:, None]
            return agg @ Wl.T + bl + x @ Wr.T
        key = jax.random.key(seed)
        ks = jax.random.split(key, 8)
        d_in, d_hid, d_out, E = (256, 512, 256, 10000)
        s = lambda k, shape, fan: jax.random.normal(k, shape, jnp.float32) * (1.0 / np.sqrt(fan))
        return {'x': jax.random.normal(ks[0], (N_NODES, d_in), jnp.float32), 'edge_index': jax.random.randint(ks[1], (2, E), 0, N_NODES, dtype=jnp.int64), 'W1l': s(ks[2], (d_hid, d_in), d_in), 'b1l': jnp.zeros((d_hid,), jnp.float32), 'W1r': s(ks[3], (d_hid, d_in), d_in), 'W2l': s(ks[4], (d_out, d_hid), d_hid), 'b2l': jnp.zeros((d_out,), jnp.float32), 'W2r': s(ks[5], (d_out, d_hid), d_hid)}
    _L1_gnn_all = _L1_gnn_setup()
    _L1_gnn_in = {k: v for k, v in _L1_gnn_all.items() if k in ('W1l', 'b1l', 'W1r', 'W2l', 'b2l', 'W2r')}
    del _L1_gnn_all

    def _L1_ffn_setup():
        import jax, jax.numpy as jnp
        import numpy as np
        B, S, H, F, E, K = (8, 128, 256, 512, 16, 2)
        EPS = 1e-05
        key = jax.random.key(seed)
        ks = jax.random.split(key, 9)
        sc = 0.02
        return {'x': jax.random.normal(ks[0], (B, S, H), dtype=jnp.float32), 'gate_w': jax.random.normal(ks[1], (H, E), dtype=jnp.float32) * sc, 'gate_b': jnp.zeros((E,), dtype=jnp.float32), 'w1': jax.random.normal(ks[2], (E, H, F), dtype=jnp.float32) * sc, 'b1': jnp.zeros((E, F), dtype=jnp.float32), 'w2': jax.random.normal(ks[3], (E, F, H), dtype=jnp.float32) * sc, 'b2': jnp.zeros((E, H), dtype=jnp.float32), 'gamma': jnp.ones((H,), dtype=jnp.float32), 'beta': jnp.zeros((H,), dtype=jnp.float32)}
    _L1_ffn_all = _L1_ffn_setup()
    _L1_ffn_in = {k: v for k, v in _L1_ffn_all.items() if k in ('gate_w', 'gate_b', 'w1', 'b1', 'w2', 'b2', 'gamma', 'beta')}
    del _L1_ffn_all
    return {'x': x, 'src': src, 'dst': dst, 'edge_weight': edge_weight, 'L0_gnn_W': _L0_gnn_in['W'], 'L0_gnn_b': _L0_gnn_in['b'], 'L0_ffn_Wg': _L0_ffn_in['Wg'], 'L0_ffn_bg': _L0_ffn_in['bg'], 'L0_ffn_W1': _L0_ffn_in['W1'], 'L0_ffn_b1': _L0_ffn_in['b1'], 'L0_ffn_W2': _L0_ffn_in['W2'], 'L0_ffn_b2': _L0_ffn_in['b2'], 'L1_gnn_W1l': _L1_gnn_in['W1l'], 'L1_gnn_b1l': _L1_gnn_in['b1l'], 'L1_gnn_W1r': _L1_gnn_in['W1r'], 'L1_gnn_W2l': _L1_gnn_in['W2l'], 'L1_gnn_b2l': _L1_gnn_in['b2l'], 'L1_gnn_W2r': _L1_gnn_in['W2r'], 'L1_ffn_gate_w': _L1_ffn_in['gate_w'], 'L1_ffn_gate_b': _L1_ffn_in['gate_b'], 'L1_ffn_w1': _L1_ffn_in['w1'], 'L1_ffn_b1': _L1_ffn_in['b1'], 'L1_ffn_w2': _L1_ffn_in['w2'], 'L1_ffn_b2': _L1_ffn_in['b2'], 'L1_ffn_gamma': _L1_ffn_in['gamma'], 'L1_ffn_beta': _L1_ffn_in['beta']}

def reference(x, src, dst, edge_weight, L0_gnn_W, L0_gnn_b, L0_ffn_Wg, L0_ffn_bg, L0_ffn_W1, L0_ffn_b1, L0_ffn_W2, L0_ffn_b2, L1_gnn_W1l, L1_gnn_b1l, L1_gnn_W1r, L1_gnn_W2l, L1_gnn_b2l, L1_gnn_W2r, L1_ffn_gate_w, L1_ffn_gate_b, L1_ffn_w1, L1_ffn_b1, L1_ffn_w2, L1_ffn_b2, L1_ffn_gamma, L1_ffn_beta):
    import jax
    import jax.numpy as jnp

    def _L0_gnn_ref(x, edge_row, edge_col, edge_val, W, b):
        import jax, jax.numpy as jnp
        import numpy as np
        N_NODES = 3125
        N_EDGES = 100000
        D_IN = 256
        D_OUT = 256
        messages = edge_val[:, None] * x[edge_col]
        agg = jax.ops.segment_sum(messages, edge_row, num_segments=N_NODES)
        return jnp.einsum('nd,od->no', agg, W) + b

    def _L0_ffn_ref(x, Wg, bg, W1, b1, W2, b2):
        import jax, jax.numpy as jnp
        import numpy as np
        B, S, D, H, E, K = (8, 256, 256, 1024, 8, 2)
        gate_scores = jnp.einsum('bsd,ed->bse', x, Wg) + bg
        topk_scores, topk_idx = jax.lax.top_k(gate_scores, K)
        topk_probs = jax.nn.softmax(topk_scores, axis=-1)
        combine = jnp.sum(topk_probs[..., None] * jax.nn.one_hot(topk_idx, E, dtype=x.dtype), axis=-2)
        out = jnp.zeros_like(x)
        for e in range(E):
            h = jax.nn.relu(jnp.einsum('bsd,hd->bsh', x, W1[e]) + b1[e])
            y = jnp.einsum('bsh,dh->bsd', h, W2[e]) + b2[e]
            out = out + combine[..., e:e + 1] * y
        return out

    def _L1_gnn_ref(x, edge_index, W1l, b1l, W1r, W2l, b2l, W2r):
        import jax, jax.numpy as jnp
        import numpy as np
        N_NODES = 3125

        def sage_conv(x, edge_index, Wl, bl, Wr):
            src, dst = (edge_index[0], edge_index[1])
            msg = x[src]
            agg = jax.ops.segment_sum(msg, dst, num_segments=N_NODES)
            cnt = jax.ops.segment_sum(jnp.ones((edge_index.shape[1],), x.dtype), dst, num_segments=N_NODES)
            agg = agg / jnp.maximum(cnt, 1.0)[:, None]
            return agg @ Wl.T + bl + x @ Wr.T
        h = sage_conv(x, edge_index, W1l, b1l, W1r)
        h = jax.nn.relu(h)
        out = sage_conv(h, edge_index, W2l, b2l, W2r)
        return out

    def _L1_ffn_ref(x, gate_w, gate_b, w1, b1, w2, b2, gamma, beta):
        import jax, jax.numpy as jnp
        import numpy as np
        B, S, H, F, E, K = (8, 128, 256, 512, 16, 2)
        EPS = 1e-05
        gate_logits = x @ gate_w + gate_b
        topk_vals, topk_idx = jax.lax.top_k(gate_logits, K)
        topk_w = jax.nn.softmax(topk_vals, axis=-1)
        h = jax.nn.relu(jnp.einsum('bsh,ehf->bsef', x, w1) + b1)
        expert_out = jnp.einsum('bsef,efh->bseh', h, w2) + b2
        sel = jnp.take_along_axis(expert_out, topk_idx[:, :, :, None], axis=2)
        moe = jnp.sum(topk_w[..., None] * sel, axis=2)
        y = x + moe
        mu = jnp.mean(y, axis=-1, keepdims=True)
        var = jnp.var(y, axis=-1, keepdims=True)
        return (y - mu) / jnp.sqrt(var + EPS) * gamma + beta
    edge_index = jnp.stack([src, dst])
    x = x + _L0_gnn_ref(_layernorm(x, axis=-1), src, dst, edge_weight, L0_gnn_W, L0_gnn_b)
    x = x + _L0_ffn_ref(_layernorm(x, axis=-1)[None], L0_ffn_Wg, L0_ffn_bg, L0_ffn_W1, L0_ffn_b1, L0_ffn_W2, L0_ffn_b2)[0]
    x = x + _L1_gnn_ref(_layernorm(x, axis=-1), edge_index, L1_gnn_W1l, L1_gnn_b1l, L1_gnn_W1r, L1_gnn_W2l, L1_gnn_b2l, L1_gnn_W2r)
    x = x + _L1_ffn_ref(_layernorm(x, axis=-1)[None], L1_ffn_gate_w, L1_ffn_gate_b, L1_ffn_w1, L1_ffn_b1, L1_ffn_w2, L1_ffn_b2, L1_ffn_gamma, L1_ffn_beta)[0]
    return x

_drawn_inputs = setup_inputs


def setup_inputs(seed=0):
    import zlib

    import numpy as np

    out = dict(_drawn_inputs(seed))
    spreads = {'L1_gnn_b1l': (0.0, 0.1),
     'L1_gnn_b2l': (0.0, 0.1),
     'L1_ffn_gate_b': (0.0, 0.37),
     'L1_ffn_b1': (0.0, 0.8),
     'L1_ffn_b2': (0.0, 0.323),
     'L1_ffn_gamma': (1.0, 0.2),
     'L1_ffn_beta': (0.0, 0.1)}
    factors = {'L0_ffn_bg': 2.808, 'L0_ffn_b1': 8.0, 'L0_ffn_b2': 6.774, 'L1_ffn_w1': 2.675}
    for name, (base, spread) in spreads.items():
        noise = np.random.default_rng([zlib.crc32(name.encode()), seed]).standard_normal(out[name].shape)
        drawn = base * np.exp(spread * noise) if base else spread * noise
        out[name] = jnp.asarray(drawn.astype(out[name].dtype))
    for name, factor in factors.items():
        out[name] = (out[name] * factor).astype(out[name].dtype)
    return out
```

```python
import concourse.bass as bass
from concourse import mybir
from contextlib import ExitStack, contextmanager

P = 128
NODES = 3125
EDGES = 53125
D = 256
NB = -(-NODES // P)
TAIL = NODES - (NB - 1) * P
EC = -(-EDGES // P)
EFULL = EDGES // EC
EREST = EDGES - EFULL * EC
UN = 8
ET = -(-((EDGES + NB * (P - 1)) // P) // UN) * UN
HID = 512
AW = D + 2
EPS = 1e-5
MOE = (dict(E=8, H=1024), dict(E=16, H=512))
for _m in MOE:
    _m["NT"] = (2 * NODES + _m["E"] * (P - 1)) // P
    _m["PER"] = 2 * D * _m["H"] // P
WB = MOE[0]["E"] * MOE[0]["PER"]
ACC0 = WB - NB * AW
RG = 5


def at_least(eng, sem, value):
    if isinstance(value, int) and value <= 0:
        return
    eng.wait_ge(sem, value)


class Chain:

    def __init__(self, eng, sem):
        self.eng, self.sem, self.base, self.n = eng, sem, 0, 0

    def link(self, ins):
        ins.then_inc(self.sem, 1)
        self.n += 1
        self.eng.wait_ge(self.sem, self.base + self.n)

    def loop(self, turn, steps):
        self.outer = self.base + self.n
        self.base, self.n, self.steps = turn * steps + self.outer, 0, steps

    def leave(self, turns):
        assert self.n == self.steps, (self.n, self.steps)
        self.base, self.n = self.outer + turns * self.steps, 0


def gnn_moe_program(nc, x, src, dst, edge_weight, l0_w, l0_b, m1_wg, m1_bg, m1_w, m1_b1, m1_b2,
                    g_w1l, g_b1l, g_w1r, g_w2, g_b2l, m2_wg, m2_bg, m2_w, m2_b1, m2_b2, gamma, beta, out):
    f32, i32 = mybir.dt.float32, mybir.dt.int32
    ALU, ACT = mybir.AluOpType, mybir.ActivationFunctionType
    ds = bass.ds

    top = ExitStack()
    with top:
        def sb(ctx, name, shape, dt=f32):
            return ctx.enter_context(nc.sbuf_tensor(name, shape, dt))

        open_sems = []

        def new_sem(name):
            open_sems.append(nc.alloc_semaphore(name))
            return open_sems[-1]

        @contextmanager
        def phase():
            with ExitStack() as ctx:
                yield ctx
            nc.clear_and_free_semaphores(open_sems)
            nc.all_engine_barrier()
            open_sems.clear()

        tab = [nc.dram_tensor(f"table{i}", (NB * P, D), f32).ap() for i in range(3)]
        rec_dram = [nc.dram_tensor(f"records{i}", ((ET + 1) * P, 4), f32).ap() for i in range(2)]
        xs_dram = [nc.dram_tensor(f"slots_x{i}", ((m["NT"] + 2) * P, D), f32).ap() for i, m in enumerate(MOE)]
        ys_dram = [nc.dram_tensor(f"slots_y{i}", (m["NT"] * P, D), f32).ap() for i, m in enumerate(MOE)]

        wbuf = sb(top, "wbuf", [P, WB])
        acc = wbuf[:, ACC0:WB]
        resid = sb(top, "resid", [P, NB * D])
        ident = sb(top, "ident", [P, P])
        tri_lt = sb(top, "tri_lt", [P, P])
        tri_le = sb(top, "tri_le", [P, P])
        iota_row = sb(top, "iota_row", [P, ET])
        iota_col = sb(top, "iota_col", [P, 1])
        ones = sb(top, "ones", [P, EC])
        stats = sb(top, "stats", [P, NB, 2])
        inv_cnt = sb(top, "inv_cnt", [P, NB])
        edge_map = [sb(top, f"edge_map{i}", [1, ET], i32) for i in range(2)]
        exp_map = [sb(top, f"exp_map{i}", [1, m["NT"]], i32) for i, m in enumerate(MOE)]
        pos_src = wbuf[:, 12288:12288 + EC].bitcast(i32)
        pos_dst = sb(top, "pos_dst", [P, EC], i32)
        rec = [wbuf[:, 10240:10240 + 4 * EC].rearrange("p (c f) -> p c f", f=4),
               sb(top, "rec1", [P, EC, 4])]
        slot = sb(top, "slot", [P, 2 * NB], i32)
        prob = sb(top, "prob", [P, 2, NB])

        banks = [top.enter_context(nc.psum_tensor(f"bank{i}", [P, 512], f32)) for i in range(8)]

        def rows(tile_ap, t, width=D):
            return tile_ap[:, ds(t * width, width)]

        def rank_dve(dve, ch, key, C, K, NT, pos, tmap, S, kcol):
            cnt, off, oh, sc, tmp, tcol = S["cnt"], S["off"], S["oh"], S["sc"], S["tmp"], S["tcol"]
            ti = S["ti"]
            with dve.Fori(0, K + 1) as k:
                ch.loop(k, 1)
                ch.link(dve.tensor_scalar(oh[:, 0:C], key, kcol[:, ds(k, 1)], None, ALU.is_equal, ALU.add,
                                          accum_out=cnt[:, ds(k, 1)]))
            ch.leave(K + 1)
            ch.link(dve.memset(tmp[:, 0:1], 0.0))
            dve.sem_inc(S["s_cnt"], 1)
            S["n_cnt"] += 1
            dve.wait_ge(S["s_tot"], S["n_cnt"] * 2 - 1)
            ch.link(dve.tensor_scalar(ti[:, 0:K], banks[0][:, 0:K], float(P - 1), None, ALU.add))
            ch.link(dve.tensor_scalar(ti[:, 0:K], ti[:, 0:K], 7, None, ALU.arith_shift_right))
            ch.link(dve.tensor_copy(tmp[:, 0:K], ti[:, 0:K]))
            ch.link(dve.tensor_tensor_scan(sc[:, 0:K], ones[:, 0:K], tmp[:, 0:K], 0.0, ALU.mult, ALU.add))
            ch.link(dve.tensor_tensor(tmp[:, 0:K], sc[:, 0:K], tmp[:, 0:K], ALU.subtract))
            ch.link(dve.tensor_scalar(off[:, 0:K], tmp[:, 0:K], float(P), -1.0, ALU.mult, ALU.add))
            ch.link(dve.memset(off[:, K:K + 1], float(NT * P - 1)))
            ch.link(dve.tensor_tensor(off[:, 0:K + 1], off[:, 0:K + 1], banks[1][:, 0:K + 1], ALU.add))
            ch.link(dve.tensor_scalar(ti[0:K, 0:1], banks[2][0:K, 0:1], float(P - 1), None, ALU.add))
            ch.link(dve.tensor_scalar(ti[0:K, 0:1], ti[0:K, 0:1], 7, None, ALU.arith_shift_right))
            dve.tensor_copy(tcol[0:K, :], ti[0:K, 0:1]).then_inc(S["s_tcol"], 1)
            ch.link(dve.memset(tmp[:, 0:C], 0.0))
            with dve.Fori(0, K + 1) as k:
                ch.loop(k, 4)
                ch.link(dve.tensor_scalar(oh[:, 0:C], key, kcol[:, ds(k, 1)], None, ALU.is_equal))
                ch.link(dve.tensor_tensor_scan(sc[:, 0:C], ones[:, 0:C], oh[:, 0:C], off[:, ds(k, 1)],
                                               ALU.mult, ALU.add))
                ch.link(dve.tensor_tensor(oh[:, 0:C], sc[:, 0:C], oh[:, 0:C], ALU.mult))
                ch.link(dve.tensor_tensor(tmp[:, 0:C], tmp[:, 0:C], oh[:, 0:C], ALU.add))
            ch.leave(K + 1)
            ch.link(dve.tensor_copy(pos, tmp[:, 0:C]))
            dve.wait_ge(S["s_tot"], S["n_cnt"] * 2)
            ch.link(dve.tensor_copy(tcol[0:K, :], banks[3][0:K, 0:1]))
            dve.tensor_scalar(oh[0:K, 0:NT], iota_row[0:K, 0:NT], tcol[0:K, :], None,
                              ALU.is_ge).then_inc(S["s_ge"], 1)
            dve.wait_ge(S["s_map"], S["n_cnt"])
            ch.link(dve.tensor_scalar(tmap[0:1, 0:NT], banks[4][0:1, 0:NT], float(K - 1), None, ALU.min))

        def rank_pe(pe, K, NT, S, n):
            cnt, tcol, oh = S["cnt"], S["tcol"], S["oh"]
            pe.wait_ge(S["s_cnt"], n)
            pe.matmul(banks[0][:, 0:K], ones[:, 0:P], cnt[:, 0:K], start=True, stop=True)
            pe.matmul(banks[1][:, 0:K + 1], tri_lt[:, :], cnt[:, 0:K + 1], start=True, stop=True)
            pe.matmul(banks[2][0:K, 0:1], cnt[:, 0:K], ones[:, 0:1], start=True, stop=True).then_inc(S["s_tot"], 1)
            pe.wait_ge(S["s_tcol"], n)
            pe.matmul(banks[3][0:K, 0:1], tri_le[0:K, 0:K], tcol[0:K, :], start=True, stop=True)\
                .then_inc(S["s_tot"], 1)
            pe.wait_ge(S["s_ge"], n)
            pe.matmul(banks[4][0:1, 0:NT], ones[0:K, 0:1], oh[0:K, 0:NT], start=True, stop=True)\
                .then_inc(S["s_map"], 1)

        def rank_scratch(ctx, tag, C, NT, region=None):
            n = max(C, NT)
            S = {}
            for i, name in enumerate(("oh", "sc", "tmp")):
                S[name] = region[:, i * n:(i + 1) * n] if region is not None else sb(ctx, f"{tag}_{name}", [P, n])
            S["cnt"], S["off"], S["tcol"] = (sb(ctx, f"{tag}_{k}", [P, w]) for k, w in
                                             (("cnt", 32), ("off", 32), ("tcol", 1)))
            S["ti"] = sb(ctx, f"{tag}_ti", [P, 32], i32)
            for k in ("s_cnt", "s_tot", "s_tcol", "s_ge", "s_map"):
                S[k] = new_sem(f"{tag}_{k}")
            S["n_cnt"] = 0
            return S

        def ln_stats_dve(dve, ch, act_sem, rt_sem, st6, n):
            rows_stats(dve, ch, resid, st6)
            dve.tensor_scalar(stats[:, :, 1], stats[:, :, 1], EPS, None, ALU.add).then_inc(act_sem, 1)
            dve.wait_ge(rt_sem, n)
            ch.link(dve.reciprocal(stats[:, :, 1], stats[:, :, 1]))

        def rows_stats(dve, ch, buf, st6):
            for t in range(NB):
                last = dve.bn_stats(st6[:, t, :], buf[:, t * D:(t + 1) * D])
            ch.link(last)
            for t in range(NB):
                last = dve.bn_aggr(stats[:, t, :], st6[:, t, :])
            ch.link(last)

        def ln_root_act(act, act_sem, rt_sem, n):
            act.wait_ge(act_sem, n)
            act.activation(stats[:, :, 1], stats[:, :, 1], ACT.Sqrt).then_inc(rt_sem, 1)

        def ln_rows_dve(dve, done):
            with dve.Fori(0, NB) as t:
                dve.tensor_scalar(rows(acc, t), rows(resid, t), stats[:, ds(t, 1), 0], stats[:, ds(t, 1), 1],
                                  ALU.subtract, ALU.mult).then_inc(done, 1)

        def table_view(table):
            return table.rearrange("(t p) d -> p t d", p=P)

        with phase() as ctx:
            sem = lambda n: new_sem(n)
            s_x, s_x2, s_e, s_iota, s_dve, s_edge, s_zero, s_fill, s_pad = (sem(n) for n in (
                "s_x", "s_x2", "s_e", "s_iota", "s_dve", "s_edge", "s_zero", "s_fill", "s_pad"))
            s_var, s_root, s_ln, s_tab = (sem(n) for n in ("s_var", "s_root", "s_ln", "s_tab"))
            ei = [sb(ctx, f"edge_i{i}", [P, EC], i32) for i in range(2)]
            ew = sb(ctx, "edge_w", [P, EC])
            S = rank_scratch(ctx, "edge", EC, ET, wbuf[:, 0:3 * ET])
            key = wbuf[:, 3 * ET:3 * ET + EC]
            tmpi = sb(ctx, "tmpi", [P, ET], i32)
            zeros = wbuf[:, 5 * ET:5 * ET + 2048]
            blank = wbuf[:, 5 * ET + 2048:5 * ET + 2048 + 4 * (ET + 1)]
            st6 = sb(ctx, "st6", [P, NB, 6])
            block = ctx.enter_context(nc.Block())

            @block.sync
            def _(sp):
                sp.wait_ge(s_pad, 1)
                for buf, arr in ((ei[0], src), (ei[1], dst), (ew, edge_weight)):
                    sp.dma_start(buf[0:EFULL, :], arr[0:EFULL * EC].rearrange("(p c) -> p c", c=EC)).then_inc(s_e, 16)
                    sp.dma_start(buf[EFULL:P, 0:EREST],
                                 arr[EFULL * EC:EDGES].rearrange("(a c) -> a c", a=1)).then_inc(s_e, 16)
                sp.dma_start(resid[:, 0:(NB - 1) * D].rearrange("p (t d) -> p t d", d=D),
                             x[0:(NB - 1) * P, :].rearrange("(t p) d -> p t d", p=P)).then_inc(s_x, 16)
                sp.dma_start(resid[0:TAIL, (NB - 1) * D:], x[(NB - 1) * P:NODES, :]).then_inc(s_x2, 16)
                sp.wait_ge(s_zero, 2)
                for r in rec_dram:
                    sp.dma_start(r.rearrange("(p a) c -> p (a c)", p=P), blank).then_inc(s_fill, 16)
                for xs in xs_dram:
                    n = xs.shape[0] * D // P
                    v = xs.rearrange("(p a) d -> p (a d)", p=P)
                    for a in range(0, n, 2048):
                        sp.dma_start(v[:, a:min(a + 2048, n)], zeros[:, 0:min(2048, n - a)]).then_inc(s_fill, 16)
                sp.wait_ge(s_ln, NB)
                sp.dma_start(table_view(tab[0]), acc[:, 0:NB * D].rearrange("p (t d) -> p t d", d=D))\
                    .then_inc(s_tab, 16)
                sp.wait_ge(s_fill, 16 * (len(rec_dram) + sum(-(-xs.shape[0] * D // P // 2048) for xs in xs_dram)))
                sp.wait_ge(s_tab, 16)

            @block.gpsimd
            def _(pool):
                pool.iota(tmpi[:, :], pattern=[[1, ET]], base=0, channel_multiplier=0).then_inc(s_iota, 1)
                pool.iota(S["ti"][:, 0:1], pattern=[[0, 1]], base=0, channel_multiplier=1).then_inc(s_iota, 1)
                pool.memset(zeros, 0.0).then_inc(s_zero, 1)

            @block.scalar
            def _(act):
                ln_root_act(act, s_var, s_root, 1)

            @block.tensor
            def _(pe):
                rank_pe(pe, NB, ET, S, 1)
                rank_pe(pe, NB, ET, S, 2)

            @block.vector
            def _(dve):
                ch = Chain(dve, s_dve)
                dve.memset(ei[0][:, :], NB * P)
                dve.memset(ei[1][:, :], NB * P)
                dve.memset(ew[:, :], 0.0)
                ch.link(dve.memset(resid[:, (NB - 1) * D:], 0.0))
                dve.sem_inc(s_pad, 1)
                b4 = blank.rearrange("p (a c) -> p a c", c=4)
                ch.link(dve.memset(blank, 0.0))
                dve.memset(b4[:, :, 2], -1.0).then_inc(s_zero, 1)
                dve.memset(ones[:, :], 1.0)
                dve.wait_ge(s_iota, 2)
                dve.tensor_copy(iota_row[:, :], tmpi[:, :])
                ch.link(dve.tensor_copy(iota_col[:, :], S["ti"][:, 0:1]))
                dve.tensor_scalar(ident[:, :], iota_row[:, 0:P], iota_col[:, :], None, ALU.is_equal)
                dve.tensor_scalar(tri_lt[:, :], iota_row[:, 0:P], iota_col[:, :], None, ALU.is_gt)
                ch.link(dve.tensor_scalar(tri_le[:, :], iota_row[:, 0:P], iota_col[:, :], None, ALU.is_ge))
                dve.wait_ge(s_e, 16 * 6)
                for i in range(2):
                    to, frm = ei[i], ei[1 - i]
                    r = rec[i]
                    ch.link(dve.tensor_scalar(r[:, :, 0].bitcast(i32), frm[:, :], float(NODES - 1), None, ALU.min))
                    if i == 0:
                        dve.tensor_copy(r[:, :, 1], ew[:, :])
                    else:
                        dve.memset(r[:, :, 1], 1.0)
                    ch.link(dve.tensor_scalar(tmpi[:, 0:EC], to[:, :], 127, None, ALU.bitwise_and))
                    ch.link(dve.tensor_copy(r[:, :, 2], tmpi[:, 0:EC]))
                    dve.memset(r[:, :, 3], 0.0)
                    ch.link(dve.tensor_scalar(tmpi[:, 0:EC], to[:, :], 7, None, ALU.arith_shift_right))
                    ch.link(dve.tensor_copy(key, tmpi[:, 0:EC]))
                    rank_dve(dve, ch, key, EC, NB, ET, (pos_src, pos_dst)[i][:, 0:EC], edge_map[i], S, iota_row)
                dve.wait_ge(s_x, 16)
                dve.wait_ge(s_x2, 16)
                ln_stats_dve(dve, ch, s_var, s_root, st6, 1)
                ln_rows_dve(dve, s_ln)

        HALF = 8
        TURNS = EC // (2 * HALF)

        def scatter_ring(ctx, tag):
            return dict(idx=sb(ctx, f"{tag}_idx", [P, 2, HALF], i32), rec=sb(ctx, f"{tag}_rec", [P, 2, HALF, 4]),
                        full=new_sem(f"{tag}_full"),
                        sent=[new_sem(f"{tag}_sent{h}") for h in range(2)])

        def scatter_dve(dve, R, i):
            pos, r = (pos_src, pos_dst)[i], rec[i]

            def turn(t):
                for h in range(2):
                    at_least(dve, R["sent"][h], t * 16 * HALF)
                    c = t * 2 * HALF + h * HALF
                    dve.tensor_copy(R["idx"][:, h, :], pos[:, ds(c, HALF)]).then_inc(R["full"], 1)
                    dve.tensor_copy(R["rec"][:, h, :, :], r[:, ds(c, HALF), :]).then_inc(R["full"], 1)

            turn(0)
            with dve.Fori(1, TURNS) as t:
                turn(t)

        def scatter_pool(pool, R, i):
            with pool.Fori(0, TURNS) as t:
                for h in range(2):
                    pool.wait_ge(R["full"], t * 4 + (2 * h + 2))
                    pool.nop(nofuse=True)
                    for j in range(HALF):
                        pool.indirect_dma_start(rec_dram[i][:, :], bass.IndirectOffsetOnAxis(R["idx"][:, h, j:j + 1], 0),
                                                R["rec"][:, h, j, :], None).then_inc(R["sent"][h], 16)
            for h in range(2):
                pool.wait_ge(R["sent"][h], TURNS * 16 * HALF)

        with phase() as ctx:
            R = scatter_ring(ctx, "sort0")
            block = ctx.enter_context(nc.Block())

            @block.vector
            def _(dve):
                scatter_dve(dve, R, 0)

            @block.gpsimd
            def _(pool):
                scatter_pool(pool, R, 0)

        def segment_sum(which, table, extra_sp, weights_done):
            with phase() as ctx:
                tag = f"seg{which}_{table.name}"
                sem = lambda n: new_sem(f"{tag}_{n}")
                recs = sb(ctx, f"{tag}_recs", [P, ET, 4])
                hot = sb(ctx, f"{tag}_hot", [P, 4, P])
                fld = sb(ctx, f"{tag}_fld", [P, 2, 4, 4])
                idx = sb(ctx, f"{tag}_idx", [P, 2, 4], i32)
                G = sb(ctx, f"{tag}_G", [P, UN, AW])
                s_rec, s_zero, s_fld, s_hot, s_seg, s_acc = (sem(n) for n in (
                    "rec", "zero", "fld", "hot", "seg", "acc"))
                s_g = [sem(f"g{b}") for b in range(UN)]
                s_w = sem("w")
                block = ctx.enter_context(nc.Block())

                @block.sync
                def _(sp):
                    sp.dma_start(recs[:, :, :], rec_dram[which][0:ET * P, :].rearrange("(t p) c -> p t c", p=P))\
                        .then_inc(s_rec, 16)
                    extra_sp(sp, s_w)

                @block.gpsimd
                def _(pool):
                    def turn(t):
                        for b in range(UN):
                            if b % 4 == 0:
                                pool.wait_ge(s_fld, t * 4 + (b // 4 * 2 + 1))
                            at_least(pool, s_seg, (t - 1) * UN + (b + 1))
                            pool.nop(nofuse=True)
                            pool.indirect_dma_start(G[:, b, 0:D], None, table[:, :],
                                                    bass.IndirectOffsetOnAxis(idx[:, b // 4, b % 4:b % 4 + 1], 0))\
                                .then_inc(s_g[b], 16)

                    turn(0)
                    with pool.Fori(1, ET // UN) as t:
                        turn(t)

                @block.vector
                def _(dve):
                    dve.memset(acc, 0.0).then_inc(s_zero, 1)
                    dve.memset(G[:, :, D:AW], 1.0).then_inc(s_zero, 1)
                    dve.wait_ge(s_zero, 2)
                    dve.wait_ge(s_rec, 16)

                    def fields(t, h):
                        for b in range(4 * h, 4 * h + 4):
                            at_least(dve, s_g[b], t * 16)
                        at_least(dve, s_hot, t * UN + 4 * h - 4)
                        r = recs[:, ds(t * UN + 4 * h, 4), :]
                        dve.tensor_copy(idx[:, h, :], r[:, :, 0].bitcast(i32)).then_inc(s_fld, 1)
                        dve.tensor_copy(fld[:, h, :, :], r).then_inc(s_fld, 1)

                    def one_hot(t, b):
                        at_least(dve, s_seg, t * UN + (b - 3))
                        dve.tensor_scalar(hot[:, b % 4, :], iota_row[:, 0:P], fld[:, b // 4, b % 4, 2:3],
                                          fld[:, b // 4, b % 4, 1:2], ALU.is_equal, ALU.mult).then_inc(s_hot, 1)

                    def add(t, b, blk):
                        dve.wait_ge(s_seg, t * UN + (b + 1))
                        at_least(dve, s_acc, t * UN + b)
                        a = acc[:, ds(blk * AW, AW)]
                        dve.tensor_tensor(a, a, banks[b % 4][:, 0:AW], ALU.add).then_inc(s_acc, 1)

                    def turn(t, more):
                        blks = [dve.value_load(edge_map[which][0:1, ds(t * UN + b, 1)], min_val=0, max_val=NB - 1)
                                for b in range(UN)]
                        for h in range(2):
                            dve.wait_ge(s_fld, t * 4 + (h * 2 + 2))
                            for b in range(4 * h, 4 * h + 4):
                                one_hot(t, b)
                                if b >= 2:
                                    add(t, b - 2, blks[b - 2])
                            if more and h == 1:
                                fields(t + 1, 0)
                        add(t, UN - 2, blks[UN - 2])
                        add(t, UN - 1, blks[UN - 1])
                        if more:
                            fields(t + 1, 1)

                    fields(0, 0)
                    fields(0, 1)
                    turn(0, True)
                    with dve.Fori(1, ET // UN - 1) as t:
                        turn(t, True)
                    turn(ET // UN - 1, False)

                @block.tensor
                def _(pe):
                    def turn(t):
                        for b in range(UN):
                            pe.wait_ge(s_g[b], t * 16 + 16)
                            pe.wait_ge(s_hot, t * UN + (b + 1))
                            at_least(pe, s_acc, t * UN + (b - 3))
                            pe.matmul(banks[b % 4][:, 0:AW], hot[:, b % 4, :], G[:, b, :], start=True, stop=True)\
                                .then_inc(s_seg, 1)

                    pe.wait_ge(s_zero, 2)
                    turn(0)
                    with pe.Fori(1, ET // UN) as t:
                        turn(t)

        def load_experts(m, w, first, last):
            per = MOE[m]["PER"]

            def load(sp, sem):
                for e in range(first, last):
                    sp.dma_start(wbuf[:, e * per:(e + 1) * per], w[e, :, :]).then_inc(sem, 16)
                sp.wait_ge(sem, 16 * (last - first))
            return load

        HEAD = [ACC0 // m["PER"] for m in MOE]
        segment_sum(0, tab[0], load_experts(0, m1_w, 0, HEAD[0]), None)

        def moe_route(m, wg, bg, pre_dve, pre_pe, pre_act, pre_sp, pre_sems):
            E, NT = MOE[m]["E"], MOE[m]["NT"]
            with phase() as ctx:
                sem = lambda n: new_sem(f"rt{m}_{n}")
                s_dve, s_var, s_root, s_ln, s_in = (sem(n) for n in ("dve", "var", "root", "ln", "in"))
                s_tp, s_tc, s_gt, s_sc, s_ex, s_exd = (sem(n) for n in ("tp", "tc", "gt", "sc", "ex", "exd"))
                s_slot, s_row, s_st = (sem(n) for n in ("slot", "row", "st"))
                stage = sb(ctx, f"rt{m}_stage", [P, D])
                S = rank_scratch(ctx, f"rt{m}", 2 * NB, NT)
                st6 = sb(ctx, f"rt{m}_st6", [P, NB, 6])
                wg_sb = sb(ctx, f"rt{m}_wg", [P, 2, E])
                bg_sb = sb(ctx, f"rt{m}_bg", [P, E])
                xT = sb(ctx, f"rt{m}_xT", [P, 2, P])
                score = sb(ctx, f"rt{m}_score", [P, NB, E])
                top8 = sb(ctx, f"rt{m}_top8", [P, NB, 8])
                ind8 = sb(ctx, f"rt{m}_ind8", [P, NB, 8], mybir.dt.uint32)
                keyf = sb(ctx, f"rt{m}_key", [P, NB, 2])
                key2 = keyf[:, :, :].rearrange("p t s -> p (t s)")
                valid = sb(ctx, f"rt{m}_valid", [P, 2])
                pre = pre_sems(ctx)
                block = ctx.enter_context(nc.Block())

                @block.sync
                def _(sp):
                    sp.dma_start(wg_sb[:, :, :], wg).then_inc(s_in, 16)
                    sp.dma_start(bg_sb[:, :], bg.partition_broadcast(P)).then_inc(s_in, 16)
                    pre_sp(sp, pre)
                    sp.wait_ge(s_in, 32)

                @block.scalar
                def _(act):
                    pre_act(act, pre, stage)
                    ln_root_act(act, s_var, s_root, 1)

                    def turn(t):
                        act.wait_ge(s_ln, t + 1)
                        at_least(act, s_tp, t)
                        act.copy(stage[:, :], rows(acc, t)).then_inc(s_st, 1)

                    turn(0)
                    with act.Fori(1, NB) as t:
                        turn(t)
                    act.wait_ge(s_ex, 1)
                    act.activation(prob[:, 1, :], prob[:, 1, :], ACT.Exp).then_inc(s_exd, 1)

                @block.tensor
                def _(pe):
                    pre_pe(pe, pre, stage)
                    pe.wait_ge(s_in, 32)

                    def turn(t):
                        pe.wait_ge(s_st, t + 1)
                        at_least(pe, s_tc, t)
                        for k in range(2):
                            mm = pe.transpose(banks[5][:, k * P:(k + 1) * P], stage[:, k * P:(k + 1) * P], ident[:, :])
                        mm.then_inc(s_tp, 1)
                        pe.wait_ge(s_tc, t + 1)
                        at_least(pe, s_sc, t)
                        for k in range(2):
                            mm = pe.matmul(banks[6][:, 0:E], xT[:, k, :], wg_sb[:, k, :], start=(k == 0), stop=(k == 1))
                        mm.then_inc(s_gt, 1)

                    turn(0)
                    with pe.Fori(1, NB) as t:
                        turn(t)
                    rank_pe(pe, E, NT, S, 1)

                @block.vector
                def _(dve):
                    ch = Chain(dve, s_dve)
                    pre_dve(dve, ch, pre)
                    ln_stats_dve(dve, ch, s_var, s_root, st6, 1)
                    ln_rows_dve(dve, s_ln)
                    dve.wait_ge(s_in, 32)

                    def turn(t):
                        dve.wait_ge(s_tp, t + 1)
                        at_least(dve, s_gt, t)
                        dve.tensor_copy(xT[:, :, :].rearrange("p k n -> p (k n)"), banks[5][:, 0:2 * P]).then_inc(s_tc, 1)
                        dve.wait_ge(s_gt, t + 1)
                        dve.tensor_tensor(score[:, ds(t, 1), :].rearrange("p a e -> p (a e)"), banks[6][:, 0:E],
                                          bg_sb[:, :], ALU.add).then_inc(s_sc, 1)

                    turn(0)
                    with dve.Fori(1, NB) as t:
                        turn(t)
                    dve.wait_ge(s_sc, NB)
                    for t in range(NB):
                        last = dve.max(top8[:, t, :], score[:, t, :])
                    ch.link(last)
                    for t in range(NB):
                        last = dve.max_index(ind8[:, t, :], top8[:, t, :], score[:, t, :])
                    ch.link(last)
                    dve.tensor_tensor(prob[:, 1, :], top8[:, :, 1], top8[:, :, 0], ALU.subtract).then_inc(s_ex, 1)
                    dve.wait_ge(s_exd, 1)
                    ch.link(dve.tensor_scalar(prob[:, 0, :], prob[:, 1, :], 1.0, None, ALU.add))
                    ch.link(dve.reciprocal(prob[:, 0, :], prob[:, 0, :]))
                    ch.link(dve.tensor_tensor(prob[:, 1, :], prob[:, 1, :], prob[:, 0, :], ALU.mult))
                    ch.link(dve.tensor_copy(keyf[:, :, :], ind8[:, :, 0:2]))
                    ch.link(dve.tensor_scalar(valid[:, 0:1], iota_col[:, :], float(TAIL), None, ALU.is_ge))
                    ch.link(dve.tensor_scalar(valid[:, 0:1], valid[:, 0:1], float(E), None, ALU.mult))
                    ch.link(dve.tensor_scalar(keyf[:, NB - 1, :], keyf[:, NB - 1, :], valid[:, 0:1], None, ALU.max))
                    rank_dve(dve, ch, key2, 2 * NB, E, NT, slot[:, :], exp_map[m], S, iota_row)
                    dve.sem_inc(s_slot, 1)

                @block.gpsimd
                def _(pool):
                    pool.wait_ge(s_slot, 1)
                    for j in range(2 * NB):
                        pool.indirect_dma_start(xs_dram[m][:, :], bass.IndirectOffsetOnAxis(slot[:, j:j + 1], 0),
                                                acc[:, j // 2 * D:(j // 2 + 1) * D], None).then_inc(s_row, 16)
                    pool.wait_ge(s_row, 2 * NB * 16)

        def moe_experts(m, load, other_dve, other_pool):
            E, H, NT, PER = (MOE[m][k] for k in ("E", "H", "NT", "PER"))
            NH, NJ = H // 512, H // P
            NG = NJ // 4
            hb, tb, yb, xb = banks[0:NH], banks[2:2 + NG], banks[4], banks[5]
            with phase() as ctx:
                sem = lambda n: new_sem(f"ff{m}_{n}")
                s_w, s_xs, s_tx, s_xt, s_up, s_h, s_th, s_ht, s_dn, s_y, s_st = (sem(n) for n in (
                    "w", "xs", "tx", "xt", "up", "h", "th", "ht", "dn", "y", "st"))
                xs = sb(ctx, f"ff{m}_xs", [P, D])
                xT = sb(ctx, f"ff{m}_xT", [P, 2, P])
                h = sb(ctx, f"ff{m}_h", [P, H])
                hT = sb(ctx, f"ff{m}_hT", [P, NJ, P])
                y = sb(ctx, f"ff{m}_y", [P, D])
                b1_sb = sb(ctx, f"ff{m}_b1", [P, E * NJ])
                b2_sb = sb(ctx, f"ff{m}_b2", [1, E * D])
                other = other_pool.ring(ctx) if other_pool else None
                block = ctx.enter_context(nc.Block())

                @block.sync
                def _(sp):
                    load(sp, s_w, b1_sb, b2_sb)

                    def fetch(t):
                        at_least(sp, s_tx, t)
                        sp.dma_start(xs[:, :], xs_dram[m][ds(t * P, P), :]).then_inc(s_xs, 16)

                    def store(t):
                        sp.wait_ge(s_y, t + 1)
                        sp.dma_start(ys_dram[m][ds(t * P, P), :], y[:, :]).then_inc(s_st, 16)

                    fetch(0)
                    fetch(1)
                    with sp.Fori(1, NT) as t:
                        fetch(t + 1)
                        store(t - 1)
                    store(NT - 1)
                    sp.wait_ge(s_xs, 16 * (NT + 1))
                    sp.wait_ge(s_st, 16 * NT)

                @block.tensor
                def _(pe):
                    def turn_x(t):
                        pe.wait_ge(s_xs, t * 16 + 16)
                        at_least(pe, s_xt, t)
                        for k in range(2):
                            mm = pe.transpose(xb[:, k * P:(k + 1) * P], xs[:, k * P:(k + 1) * P], ident[:, :])
                        mm.then_inc(s_tx, 1)

                    def up(t, e):
                        pe.wait_ge(s_xt, t + 1)
                        at_least(pe, s_h, t * NH)
                        for n in range(NH):
                            for k in range(2):
                                mm = pe.matmul(hb[n][:, :], xT[:, k, :],
                                               wbuf[:, ds(e * PER + (k * H + n * 512), 512)],
                                               start=(k == 0), stop=(k == 1))
                            mm.then_inc(s_up, 1)

                    def turn_h(t):
                        pe.wait_ge(s_h, t * NH + NH)
                        at_least(pe, s_ht, t * NG)
                        for g in range(NG):
                            for j in range(4):
                                mm = pe.transpose(tb[g][:, j * P:(j + 1) * P],
                                                  h[:, (4 * g + j) * P:(4 * g + j + 1) * P], ident[:, :])
                            mm.then_inc(s_th, 1)

                    def down(t, e):
                        pe.wait_ge(s_ht, t * NG + NG)
                        at_least(pe, s_y, t)
                        pe.matmul(yb[:, 0:D], ones[0:1, 0:P], b2_sb[0:1, ds(e * D, D)], start=True, stop=False)
                        for j in range(NJ):
                            mm = pe.matmul(yb[:, 0:D], hT[:, j, :], wbuf[:, ds(e * PER + (2 * H + j * D), D)],
                                           start=False, stop=(j == NJ - 1))
                        mm.then_inc(s_dn, 1)

                    def expert(t):
                        return pe.value_load(exp_map[m][0:1, ds(t, 1)], min_val=0, max_val=E - 1)

                    pe.wait_ge(s_w, W_LOADS * 16)
                    turn_x(0)
                    up(0, expert(0))
                    turn_x(1)
                    turn_h(0)
                    with pe.Fori(1, NT) as t:
                        up(t, expert(t))
                        turn_x(t + 1)
                        down(t - 1, expert(t - 1))
                        turn_h(t)
                    down(NT - 1, expert(NT - 1))

                @block.scalar
                def _(act):
                    act.wait_ge(s_w, W_LOADS * 16)

                    def turn(t):
                        e = act.value_load(exp_map[m][0:1, ds(t, 1)], min_val=0, max_val=E - 1)
                        for g in range(NG):
                            act.wait_ge(s_th, t * NG + (g + 1))
                            at_least(act, s_dn, t)
                            for j in range(4):
                                q = 4 * g + j
                                last = act.activation(hT[:, q, :], tb[g][:, j * P:(j + 1) * P], ACT.Relu,
                                                      bias=b1_sb[:, ds(e * NJ + q, 1)])
                            last.then_inc(s_ht, 1)

                    turn(0)
                    with act.Fori(1, NT) as t:
                        turn(t)

                @block.vector
                def _(dve):
                    def copy_x(t):
                        dve.wait_ge(s_tx, t + 1)
                        at_least(dve, s_up, t * NH)
                        dve.tensor_copy(xT[:, :, :].rearrange("p k n -> p (k n)"), xb[:, 0:2 * P]).then_inc(s_xt, 1)

                    def copy_h(t):
                        at_least(dve, s_th, t * NG)
                        for n in range(NH):
                            dve.wait_ge(s_up, t * NH + (n + 1))
                            dve.tensor_copy(h[:, n * 512:(n + 1) * 512], hb[n][:, :]).then_inc(s_h, 1)

                    def copy_y(t):
                        dve.wait_ge(s_dn, t + 1)
                        at_least(dve, s_st, t * 16)
                        dve.tensor_copy(y[:, :], yb[:, 0:D]).then_inc(s_y, 1)

                    copy_x(0)
                    copy_h(0)
                    copy_x(1)
                    with dve.Fori(1, NT) as t:
                        copy_h(t)
                        copy_x(t + 1)
                        copy_y(t - 1)
                        if other_pool:
                            other_dve(dve, other, t)
                    copy_y(NT - 1)

                if other_pool:
                    @block.gpsimd
                    def _(pool):
                        other_pool(pool, other)

        def moe_combine(m, post_dve, post_act, post_sp, post_sems):
            target = resid if m == 0 else acc
            with phase() as ctx:
                sem = lambda n: new_sem(f"cb{m}_{n}")
                s_idx, s_use, s_add, s_dve, s_pre = (sem(n) for n in ("idx", "use", "add", "dve", "pre"))
                s_g = [sem(f"g{j}") for j in range(2 * RG)]
                Y = sb(ctx, f"cb{m}_Y", [P, 2 * RG, D])
                idx = sb(ctx, f"cb{m}_idx", [P, 2 * NB], i32)
                post = post_sems(ctx)
                block = ctx.enter_context(nc.Block())

                @block.gpsimd
                def _(pool):
                    for j in range(2 * NB):
                        b = j % (2 * RG)
                        if j >= 2 * RG:
                            pool.wait_ge(s_add, j - 2 * RG + 1)
                        if j == 0:
                            pool.wait_ge(s_idx, 1)
                        pool.indirect_dma_start(Y[:, b, :], None, ys_dram[m][:, :],
                                                bass.IndirectOffsetOnAxis(idx[:, j:j + 1], 0)).then_inc(s_g[b], 16)

                @block.vector
                def _(dve):
                    ch = Chain(dve, s_dve)
                    dve.tensor_scalar(idx[:, :], slot[:, :], float(MOE[m]["NT"] * P - 1), None, ALU.min)\
                        .then_inc(s_idx, 1)
                    if m == 1:
                        ln_rows_dve(dve, s_pre)
                        dve.wait_ge(s_pre, NB)

                    def turn(t):
                        for j in range(2 * RG):
                            dve.wait_ge(s_g[j], t * 16 + 16)
                            r = target[:, ds((t * RG + j // 2) * D, D)]
                            if j % 2:
                                dve.wait_ge(s_add, t * 2 * RG + j)
                            dve.scalar_tensor_tensor(r, Y[:, j, :], prob[:, j % 2, ds(t * RG + j // 2, 1)], r,
                                                     ALU.mult, ALU.add).then_inc(s_add, 1)

                    turn(0)
                    with dve.Fori(1, NB // RG) as t:
                        turn(t)
                    dve.wait_ge(s_add, 2 * NB)
                    post_dve(dve, ch, post)

                @block.scalar
                def _(act):
                    post_act(act, post)

                @block.sync
                def _(sp):
                    post_sp(sp, post)

        def pre0_sems(ctx):
            p = {k: new_sem(f"l0_{k}") for k in ("w", "st", "tp", "tc", "mm", "up")}
            p["W"] = sb(ctx, "l0_W", [P, 2, D])
            p["B"] = sb(ctx, "l0_B", [P, D])
            p["T"] = sb(ctx, "l0_T", [P, 2, P])
            return p

        def pre0_sp(sp, p):
            sp.dma_start(p["W"][:, :, :], l0_w).then_inc(p["w"], 16)
            sp.dma_start(p["B"][:, :], l0_b.partition_broadcast(P)).then_inc(p["w"], 16)

        def pre0_act(act, p, stage):
            def turn(t):
                at_least(act, p["tp"], t)
                act.copy(stage[:, :], acc[:, ds(t * AW, D)]).then_inc(p["st"], 1)

            turn(0)
            with act.Fori(1, NB) as t:
                turn(t)
            act.wait_ge(p["tp"], NB)

        def pre0_pe(pe, p, stage):
            pe.wait_ge(p["w"], 32)

            def turn(t):
                pe.wait_ge(p["st"], t + 1)
                at_least(pe, p["tc"], t)
                for k in range(2):
                    mm = pe.transpose(banks[0][:, k * P:(k + 1) * P], stage[:, k * P:(k + 1) * P], ident[:, :])
                mm.then_inc(p["tp"], 1)
                pe.wait_ge(p["tc"], t + 1)
                at_least(pe, p["up"], t)
                for k in range(2):
                    mm = pe.matmul(banks[1][:, 0:D], p["T"][:, k, :], p["W"][:, k, :], start=(k == 0), stop=(k == 1))
                mm.then_inc(p["mm"], 1)

            turn(0)
            with pe.Fori(1, NB) as t:
                turn(t)

        def pre0_dve(dve, ch, p):
            dve.wait_ge(p["w"], 32)

            def turn(t):
                dve.wait_ge(p["tp"], t + 1)
                at_least(dve, p["mm"], t)
                dve.tensor_copy(p["T"][:, :, :].rearrange("p k n -> p (k n)"), banks[0][:, 0:2 * P]).then_inc(p["tc"], 1)
                ch.link(dve.tensor_tensor(rows(resid, t), rows(resid, t), p["B"][:, :], ALU.add))
                dve.wait_ge(p["mm"], t + 1)
                dve.tensor_tensor(rows(resid, t), rows(resid, t), banks[1][:, 0:D], ALU.add).then_inc(p["up"], 1)

            ch.loop(0, 1)
            turn(0)
            ch.leave(1)
            with dve.Fori(1, NB) as t:
                ch.loop(t - 1, 1)
                turn(t)
            ch.leave(NB - 1)
            dve.wait_ge(p["up"], NB)

        moe_route(0, m1_wg, m1_bg, pre0_dve, pre0_pe, pre0_act, pre0_sp, pre0_sems)

        W_LOADS = MOE[0]["E"] - HEAD[0] + 2

        def load0(sp, sem, b1_sb, b2_sb):
            per = MOE[0]["PER"]
            for e in range(HEAD[0], MOE[0]["E"]):
                sp.dma_start(wbuf[:, e * per:(e + 1) * per], m1_w[e, :, :]).then_inc(sem, 16)
            sp.dma_start(b1_sb[:, :], m1_b1).then_inc(sem, 16)
            sp.dma_start(b2_sb[:, :], m1_b2).then_inc(sem, 16)

        def sort1_dve(dve, R, t):
            pass

        class Sort1:
            ring = staticmethod(lambda ctx: scatter_ring(ctx, "sort1"))

            def __call__(self, pool, R):
                scatter_pool(pool, R, 1)

        def sort1_step(dve, R, t):
            pass

        moe_experts(0, load0, None, None)

        with phase() as ctx:
            R = scatter_ring(ctx, "sort1")
            block = ctx.enter_context(nc.Block())

            @block.vector
            def _(dve):
                scatter_dve(dve, R, 1)

            @block.gpsimd
            def _(pool):
                scatter_pool(pool, R, 1)

        def post0_sems(ctx):
            p = {k: new_sem(f"post0_{k}") for k in ("var", "root", "ln", "tab")}
            p["st6"] = sb(ctx, "post0_st6", [P, NB, 6])
            return p

        def post0_dve(dve, ch, p):
            ln_stats_dve(dve, ch, p["var"], p["root"], p["st6"], 1)
            ln_rows_dve(dve, p["ln"])

        def post0_act(act, p):
            ln_root_act(act, p["var"], p["root"], 1)

        def post0_sp(sp, p):
            sp.wait_ge(p["ln"], NB)
            sp.dma_start(table_view(tab[1]), acc[:, 0:NB * D].rearrange("p (t d) -> p t d", d=D)).then_inc(p["tab"], 16)
            sp.wait_ge(p["tab"], 16)

        moe_combine(0, post0_dve, post0_act, post0_sp, post0_sems)

        segment_sum(1, tab[1], load_experts(1, m2_w, 0, HEAD[1]), None)

        with phase() as ctx:
            sem = lambda n: new_sem(f"sage_{n}")
            s_w, s_dve, s_in, s_tp, s_tc, s_m1, s_h, s_th, s_ht, s_m2, s_z, s_st = (sem(n) for n in (
                "w", "dve", "in", "tp", "tc", "m1", "h", "th", "ht", "m2", "z", "st"))
            W1 = sb(ctx, "sage_W1", [P, 4, HID])
            W2 = sb(ctx, "sage_W2", [P, 4, 2 * D])
            B1 = sb(ctx, "sage_B1", [P, HID])
            B2 = sb(ctx, "sage_B2", [P, D])
            mx = sb(ctx, "sage_mx", [P, 2, D])
            mxT = sb(ctx, "sage_mxT", [P, 4, P])
            h = sb(ctx, "sage_h", [P, HID])
            hT = sb(ctx, "sage_hT", [P, 4, P])
            z = sb(ctx, "sage_z", [P, D])
            accv = acc.rearrange("p (t a) -> p t a", a=AW)
            block = ctx.enter_context(nc.Block())

            @block.sync
            def _(sp):
                sp.dma_start(W1[:, 0:2, :], g_w1l).then_inc(s_w, 16)
                sp.dma_start(W1[:, 2:4, :], g_w1r).then_inc(s_w, 16)
                sp.dma_start(W2[:, :, :], g_w2).then_inc(s_w, 16)
                sp.dma_start(B1[:, :], g_b1l.partition_broadcast(P)).then_inc(s_w, 16)
                sp.dma_start(B2[:, :], g_b2l.partition_broadcast(P)).then_inc(s_w, 16)
                with sp.Fori(0, NB) as t:
                    sp.wait_ge(s_z, t * 2 + 1)
                    sp.dma_start(tab[2][ds(t * P, P), :], z[:, :]).then_inc(s_st, 16)
                sp.wait_ge(s_st, NB * 16)

            @block.tensor
            def _(pe):
                pe.wait_ge(s_w, 80)

                def turn(t):
                    pe.wait_ge(s_in, t * 2 + 2)
                    at_least(pe, s_tc, t)
                    for q in range(4):
                        mm = pe.transpose(banks[0][:, q * P:(q + 1) * P],
                                          mx[:, q // 2, (q % 2) * P:(q % 2 + 1) * P], ident[:, :])
                    mm.then_inc(s_tp, 1)
                    pe.wait_ge(s_tc, t + 1)
                    at_least(pe, s_h, t)
                    for q in range(4):
                        mm = pe.matmul(banks[1][:, :], mxT[:, q, :], W1[:, q, :], start=(q == 0), stop=(q == 3))
                    mm.then_inc(s_m1, 1)
                    pe.wait_ge(s_h, t + 1)
                    at_least(pe, s_ht, t)
                    for q in range(4):
                        mm = pe.transpose(banks[2][:, q * P:(q + 1) * P], h[:, q * P:(q + 1) * P], ident[:, :])
                    mm.then_inc(s_th, 1)
                    pe.wait_ge(s_ht, t + 1)
                    at_least(pe, s_z, t * 2)
                    for q in range(4):
                        mm = pe.matmul(banks[3][:, :], hT[:, q, :], W2[:, q, :], start=(q == 0), stop=(q == 3))
                    mm.then_inc(s_m2, 1)

                turn(0)
                with pe.Fori(1, NB) as t:
                    turn(t)

            @block.scalar
            def _(act):
                def turn(t):
                    act.wait_ge(s_tp, t + 1)
                    at_least(act, s_m1, t)
                    act.activation(mxT[:, :, :].rearrange("p k n -> p (k n)"), banks[0][:, :], ACT.Copy).then_inc(s_tc, 1)
                    act.wait_ge(s_th, t + 1)
                    at_least(act, s_m2, t)
                    act.activation(hT[:, :, :].rearrange("p k n -> p (k n)"), banks[2][:, :], ACT.Relu).then_inc(s_ht, 1)

                turn(0)
                with act.Fori(1, NB) as t:
                    turn(t)

            @block.vector
            def _(dve):
                ch = Chain(dve, s_dve)
                dve.wait_ge(s_w, 80)
                ch.link(dve.tensor_scalar(inv_cnt[:, :], accv[:, :, D], 1.0, None, ALU.max))
                ch.link(dve.reciprocal(inv_cnt[:, :], inv_cnt[:, :]))

                def turn(t):
                    at_least(dve, s_tp, t)
                    dve.tensor_scalar(mx[:, 0, :], acc[:, ds(t * AW, D)], inv_cnt[:, ds(t, 1)], None, ALU.mult)\
                        .then_inc(s_in, 1)
                    dve.tensor_scalar(mx[:, 1, :], rows(resid, t), stats[:, ds(t, 1), 0], stats[:, ds(t, 1), 1],
                                      ALU.subtract, ALU.mult).then_inc(s_in, 1)
                    dve.wait_ge(s_in, t * 2 + 2)
                    ch.link(dve.tensor_tensor(rows(resid, t), rows(resid, t), B2[:, :], ALU.add))
                    dve.wait_ge(s_m1, t + 1)
                    at_least(dve, s_th, t)
                    dve.tensor_tensor(h[:, :], banks[1][:, :], B1[:, :], ALU.add).then_inc(s_h, 1)
                    dve.wait_ge(s_m2, t + 1)
                    at_least(dve, s_st, t * 16)
                    dve.tensor_copy(z[:, :], banks[3][:, 0:D]).then_inc(s_z, 1)
                    dve.tensor_tensor(rows(resid, t), rows(resid, t), banks[3][:, D:2 * D], ALU.add).then_inc(s_z, 1)

                ch.loop(0, 1)
                turn(0)
                ch.leave(1)
                with dve.Fori(1, NB) as t:
                    ch.loop(t - 1, 1)
                    turn(t)
                ch.leave(NB - 1)

        segment_sum(1, tab[2], lambda sp, sem: None, None)

        def pre1_sems(ctx):
            return dict(up=new_sem("pre1_up"))

        def pre1_dve(dve, ch, p):
            with dve.Fori(0, NB) as t:
                dve.scalar_tensor_tensor(rows(resid, t), acc[:, ds(t * AW, D)], inv_cnt[:, ds(t, 1)],
                                         rows(resid, t), ALU.mult, ALU.add).then_inc(p["up"], 1)
            dve.wait_ge(p["up"], NB)

        moe_route(1, m2_wg, m2_bg, pre1_dve, lambda pe, p, s: None, lambda act, p, s: None, lambda sp, p: None, pre1_sems)

        W_LOADS = MOE[1]["E"] - HEAD[1] + 2

        def load1(sp, sem, b1_sb, b2_sb):
            per = MOE[1]["PER"]
            for e in range(HEAD[1], MOE[1]["E"]):
                sp.dma_start(wbuf[:, e * per:(e + 1) * per], m2_w[e, :, :]).then_inc(sem, 16)
            sp.dma_start(b1_sb[:, :], m2_b1).then_inc(sem, 16)
            sp.dma_start(b2_sb[:, :], m2_b2).then_inc(sem, 16)

        moe_experts(1, load1, None, None)

        def post1_sems(ctx):
            p = {k: new_sem(f"post1_{k}") for k in ("w", "var", "root", "up", "out")}
            p["st6"] = sb(ctx, "post1_st6", [P, NB, 6])
            p["G"] = sb(ctx, "post1_G", [P, D])
            p["B"] = sb(ctx, "post1_B", [P, D])
            return p

        def post1_dve(dve, ch, p):
            rows_stats(dve, ch, acc, p["st6"])
            dve.tensor_scalar(stats[:, :, 1], stats[:, :, 1], EPS, None, ALU.add).then_inc(p["var"], 1)
            dve.wait_ge(p["root"], 1)
            ch.link(dve.reciprocal(stats[:, :, 1], stats[:, :, 1]))
            dve.wait_ge(p["w"], 32)
            with dve.Fori(0, NB) as t:
                ch.loop(t, 3)
                a = rows(acc, t)
                ch.link(dve.tensor_scalar(a, a, stats[:, ds(t, 1), 0], stats[:, ds(t, 1), 1],
                                          ALU.subtract, ALU.mult))
                ch.link(dve.tensor_tensor(a, a, p["G"][:, :], ALU.mult))
                ch.link(dve.tensor_tensor(a, a, p["B"][:, :], ALU.add))
                dve.tensor_tensor(rows(resid, t), rows(resid, t), a, ALU.add).then_inc(p["up"], 1)
            ch.leave(NB)

        def post1_act(act, p):
            ln_root_act(act, p["var"], p["root"], 1)

        def post1_sp(sp, p):
            sp.dma_start(p["G"][:, :], gamma.partition_broadcast(P)).then_inc(p["w"], 16)
            sp.dma_start(p["B"][:, :], beta.partition_broadcast(P)).then_inc(p["w"], 16)
            with sp.Fori(0, NB - 1) as t:
                sp.wait_ge(p["up"], t + 1)
                sp.dma_start(out[ds(t * P, P), :], rows(resid, t)).then_inc(p["out"], 16)
            sp.wait_ge(p["up"], NB)
            sp.dma_start(out[(NB - 1) * P:NODES, :], resid[0:TAIL, (NB - 1) * D:]).then_inc(p["out"], 16)
            sp.wait_ge(p["out"], NB * 16)

        moe_combine(1, post1_dve, post1_act, post1_sp, post1_sems)


def kernel(**inputs):
    import numpy as _np
    import concourse.bacc as _bacc
    from concourse import mybir as _mybir
    from concourse.bass_utils import run_bass_kernel_spmd as _run

    def up(a, *order):
        a = _np.transpose(_np.asarray(a), order) if order else _np.asarray(a)
        return a.reshape(a.shape[0] // 128, 128, -1).transpose(1, 0, 2)

    def experts(w_up, w_down):
        parts = [w.reshape(w.shape[0], w.shape[1] // 128, 128, -1).transpose(0, 2, 1, 3).reshape(w.shape[0], 128, -1)
                 for w in (w_up, w_down)]
        return _np.concatenate(parts, axis=2)

    g = {k: _np.asarray(v) for k, v in inputs.items()}
    args = dict(
        x=g["x"], src=g["src"], dst=g["dst"], edge_weight=g["edge_weight"],
        l0_w=up(g["L0_gnn_W"], 1, 0), l0_b=g["L0_gnn_b"],
        m1_wg=up(g["L0_ffn_Wg"], 1, 0), m1_bg=g["L0_ffn_bg"],
        m1_w=experts(g["L0_ffn_W1"].transpose(0, 2, 1), g["L0_ffn_W2"].transpose(0, 2, 1)),
        m1_b1=g["L0_ffn_b1"].reshape(8 * 8, 128).T, m1_b2=g["L0_ffn_b2"].reshape(1, -1),
        g_w1l=up(g["L1_gnn_W1l"], 1, 0), g_b1l=g["L1_gnn_b1l"], g_w1r=up(g["L1_gnn_W1r"], 1, 0),
        g_w2=_np.concatenate([up(g["L1_gnn_W2l"], 1, 0), up(g["L1_gnn_W2r"], 1, 0)], axis=2),
        g_b2l=g["L1_gnn_b2l"],
        m2_wg=up(g["L1_ffn_gate_w"]), m2_bg=g["L1_ffn_gate_b"], m2_w=experts(g["L1_ffn_w1"], g["L1_ffn_w2"]),
        m2_b1=g["L1_ffn_b1"].reshape(16 * 4, 128).T, m2_b2=g["L1_ffn_b2"].reshape(1, -1),
        gamma=g["L1_ffn_gamma"], beta=g["L1_ffn_beta"])
    nc = _bacc.Bacc("TRN2", target_bir_lowering=False, num_devices=1)
    arrays, aps = {}, {}
    for name, a in args.items():
        a = _np.ascontiguousarray(a)
        arrays[f"in_{name}"] = a
        aps[name] = nc.dram_tensor(f"in_{name}", a.shape, _mybir.dt.from_np(a.dtype), kind="ExternalInput").ap()
    aps["out"] = nc.dram_tensor("out_0", (3125, 256), _mybir.dt.float32, kind="ExternalOutput").ap()
    gnn_moe_program(nc, **aps)
    r = _run(nc, [arrays], core_ids=[0])
    return r.results[0]["out_0"]
```

```python
import concourse.bass as bass
from concourse import mybir
from contextlib import ExitStack, contextmanager

P = 128
NODES = 3125
EDGES = 53125
D = 256
NB = -(-NODES // P)
TAIL = NODES - (NB - 1) * P
EC = -(-EDGES // P)
EFULL = EDGES // EC
EREST = EDGES - EFULL * EC
UN = 8
ET = -(-((EDGES + NB * (P - 1)) // P) // UN) * UN
HID = 512
AW = D + 2
EPS = 1e-5
MOE = (dict(E=8, H=1024), dict(E=16, H=512))
for _m in MOE:
    _m["NT"] = (2 * NODES + _m["E"] * (P - 1)) // P
    _m["PER"] = 2 * D * _m["H"] // P
WB = MOE[0]["E"] * MOE[0]["PER"]
ACC0 = WB - NB * AW
RG = 5


def at_least(eng, sem, value):
    if isinstance(value, int) and value <= 0:
        return
    eng.wait_ge(sem, value)


class Chain:

    def __init__(self, eng, sem):
        self.eng, self.sem, self.base, self.n = eng, sem, 0, 0

    def link(self, ins):
        ins.then_inc(self.sem, 1)
        self.n += 1
        self.eng.wait_ge(self.sem, self.base + self.n)

    def loop(self, turn, steps):
        self.outer = self.base + self.n
        self.base, self.n, self.steps = turn * steps + self.outer, 0, steps

    def leave(self, turns):
        assert self.n == self.steps, (self.n, self.steps)
        self.base, self.n = self.outer + turns * self.steps, 0


def gnn_moe_program(nc, x, src, dst, edge_weight, l0_w, l0_b, m1_wg, m1_bg, m1_w, m1_b1, m1_b2,
                    g_w1l, g_b1l, g_w1r, g_w2, g_b2l, m2_wg, m2_bg, m2_w, m2_b1, m2_b2, gamma, beta, out):
    f32, i32 = mybir.dt.float32, mybir.dt.int32
    ALU, ACT = mybir.AluOpType, mybir.ActivationFunctionType
    ds = bass.ds
    DVE = mybir.EngineType.DVE

    top = ExitStack()
    with top:
        def sb(ctx, name, shape, dt=f32):
            return ctx.enter_context(nc.sbuf_tensor(name, shape, dt))

        open_sems = []

        def new_sem(name):
            open_sems.append(nc.alloc_semaphore(name))
            return open_sems[-1]

        @contextmanager
        def phase():
            with ExitStack() as ctx:
                yield ctx
            nc.clear_and_free_semaphores(open_sems)
            nc.all_engine_barrier()
            open_sems.clear()

        tab = [nc.dram_tensor(f"table{i}", (NB * P, D), f32).ap() for i in range(3)]
        rec_dram = [nc.dram_tensor(f"records{i}", ((ET + 1) * P, 4), f32).ap() for i in range(2)]
        xs_dram = [nc.dram_tensor(f"slots_x{i}", ((m["NT"] + 2) * P, D), f32).ap() for i, m in enumerate(MOE)]
        ys_dram = [nc.dram_tensor(f"slots_y{i}", (m["NT"] * P, D), f32).ap() for i, m in enumerate(MOE)]

        wbuf = sb(top, "wbuf", [P, WB])
        acc = wbuf[:, ACC0:WB]
        resid = sb(top, "resid", [P, NB * D])
        ident = sb(top, "ident", [P, P])
        tri_lt = sb(top, "tri_lt", [P, P])
        tri_le = sb(top, "tri_le", [P, P])
        iota_row = sb(top, "iota_row", [P, ET])
        iota_col = sb(top, "iota_col", [P, 1])
        ones = sb(top, "ones", [P, EC])
        stats = sb(top, "stats", [P, NB, 2])
        inv_cnt = sb(top, "inv_cnt", [P, NB])
        edge_map = [sb(top, f"edge_map{i}", [1, ET], i32) for i in range(2)]
        exp_map = [sb(top, f"exp_map{i}", [1, m["NT"]], i32) for i, m in enumerate(MOE)]
        pos_src = wbuf[:, 12288:12288 + EC].bitcast(i32)
        pos_dst = sb(top, "pos_dst", [P, EC], i32)
        rec = [wbuf[:, 10240:10240 + 4 * EC].rearrange("p (c f) -> p c f", f=4),
               sb(top, "rec1", [P, EC, 4])]
        slot = sb(top, "slot", [P, 2 * NB], i32)
        prob = sb(top, "prob", [P, 2, NB])

        banks = [top.enter_context(nc.psum_tensor(f"bank{i}", [P, 512], f32)) for i in range(8)]

        def rows(tile_ap, t, width=D):
            return tile_ap[:, ds(t * width, width)]

        def rank_dve(dve, ch, key, C, K, NT, pos, tmap, S, kcol):
            cnt, off, oh, sc, tmp, tcol = S["cnt"], S["off"], S["oh"], S["sc"], S["tmp"], S["tcol"]
            ti = S["ti"]
            with dve.Fori(0, K + 1) as k:
                ch.loop(k, 1)
                ch.link(dve.tensor_scalar(oh[:, 0:C], key, kcol[:, ds(k, 1)], None, ALU.is_equal, ALU.add,
                                          accum_out=cnt[:, ds(k, 1)]))
            ch.leave(K + 1)
            ch.link(dve.memset(tmp[:, 0:1], 0.0))
            dve.sem_inc(S["s_cnt"], 1)
            S["n_cnt"] += 1
            dve.wait_ge(S["s_tot"], S["n_cnt"] * 2 - 1)
            ch.link(dve.tensor_scalar(ti[:, 0:K], banks[0][:, 0:K], float(P - 1), None, ALU.add))
            ch.link(dve.tensor_scalar(ti[:, 0:K], ti[:, 0:K], 7, None, ALU.arith_shift_right))
            ch.link(dve.tensor_copy(tmp[:, 0:K], ti[:, 0:K]))
            ch.link(dve.tensor_tensor_scan(sc[:, 0:K], ones[:, 0:K], tmp[:, 0:K], 0.0, ALU.mult, ALU.add))
            ch.link(dve.tensor_tensor(tmp[:, 0:K], sc[:, 0:K], tmp[:, 0:K], ALU.subtract))
            ch.link(dve.tensor_scalar(off[:, 0:K], tmp[:, 0:K], float(P), -1.0, ALU.mult, ALU.add))
            ch.link(dve.memset(off[:, K:K + 1], float(NT * P - 1)))
            ch.link(dve.tensor_tensor(off[:, 0:K + 1], off[:, 0:K + 1], banks[1][:, 0:K + 1], ALU.add))
            ch.link(dve.tensor_scalar(ti[0:K, 0:1], banks[2][0:K, 0:1], float(P - 1), None, ALU.add))
            ch.link(dve.tensor_scalar(ti[0:K, 0:1], ti[0:K, 0:1], 7, None, ALU.arith_shift_right))
            dve.tensor_copy(tcol[0:K, :], ti[0:K, 0:1]).then_inc(S["s_tcol"], 1)
            ch.link(dve.memset(tmp[:, 0:C], 0.0))
            with dve.Fori(0, K + 1) as k:
                ch.loop(k, 4)
                ch.link(dve.tensor_scalar(oh[:, 0:C], key, kcol[:, ds(k, 1)], None, ALU.is_equal))
                ch.link(dve.tensor_tensor_scan(sc[:, 0:C], ones[:, 0:C], oh[:, 0:C], off[:, ds(k, 1)],
                                               ALU.mult, ALU.add))
                ch.link(dve.tensor_tensor(oh[:, 0:C], sc[:, 0:C], oh[:, 0:C], ALU.mult))
                ch.link(dve.tensor_tensor(tmp[:, 0:C], tmp[:, 0:C], oh[:, 0:C], ALU.add))
            ch.leave(K + 1)
            ch.link(dve.tensor_copy(pos, tmp[:, 0:C]))
            dve.wait_ge(S["s_tot"], S["n_cnt"] * 2)
            ch.link(dve.tensor_copy(tcol[0:K, :], banks[3][0:K, 0:1]))
            dve.tensor_scalar(oh[0:K, 0:NT], iota_row[0:K, 0:NT], tcol[0:K, :], None,
                              ALU.is_ge).then_inc(S["s_ge"], 1)
            dve.wait_ge(S["s_map"], S["n_cnt"])
            ch.link(dve.tensor_scalar(tmap[0:1, 0:NT], banks[4][0:1, 0:NT], float(K - 1), None, ALU.min))

        def rank_pe(pe, K, NT, S, n):
            cnt, tcol, oh = S["cnt"], S["tcol"], S["oh"]
            pe.wait_ge(S["s_cnt"], n)
            pe.matmul(banks[0][:, 0:K], ones[:, 0:P], cnt[:, 0:K], start=True, stop=True)
            pe.matmul(banks[1][:, 0:K + 1], tri_lt[:, :], cnt[:, 0:K + 1], start=True, stop=True)
            pe.matmul(banks[2][0:K, 0:1], cnt[:, 0:K], ones[:, 0:1], start=True, stop=True).then_inc(S["s_tot"], 1)
            pe.wait_ge(S["s_tcol"], n)
            pe.matmul(banks[3][0:K, 0:1], tri_le[0:K, 0:K], tcol[0:K, :], start=True, stop=True)\
                .then_inc(S["s_tot"], 1)
            pe.wait_ge(S["s_ge"], n)
            pe.matmul(banks[4][0:1, 0:NT], ones[0:K, 0:1], oh[0:K, 0:NT], start=True, stop=True)\
                .then_inc(S["s_map"], 1)

        def rank_scratch(ctx, tag, C, NT, region=None):
            n = max(C, NT)
            S = {}
            for i, name in enumerate(("oh", "sc", "tmp")):
                S[name] = region[:, i * n:(i + 1) * n] if region is not None else sb(ctx, f"{tag}_{name}", [P, n])
            S["cnt"], S["off"], S["tcol"] = (sb(ctx, f"{tag}_{k}", [P, w]) for k, w in
                                             (("cnt", 32), ("off", 32), ("tcol", 1)))
            S["ti"] = sb(ctx, f"{tag}_ti", [P, 32], i32)
            for k in ("s_cnt", "s_tot", "s_tcol", "s_ge", "s_map"):
                S[k] = new_sem(f"{tag}_{k}")
            S["n_cnt"] = 0
            return S

        def ln_stats_dve(dve, ch, act_sem, rt_sem, st6, n):
            rows_stats(dve, ch, resid, st6)
            dve.tensor_scalar(stats[:, :, 1], stats[:, :, 1], EPS, None, ALU.add).then_inc(act_sem, 1)
            dve.wait_ge(rt_sem, n)
            ch.link(dve.reciprocal(stats[:, :, 1], stats[:, :, 1]))

        def rows_stats(dve, ch, buf, st6):
            for t in range(NB):
                last = dve.bn_stats(st6[:, t, :], buf[:, t * D:(t + 1) * D])
            ch.link(last)
            for t in range(NB):
                last = dve.bn_aggr(stats[:, t, :], st6[:, t, :])
            ch.link(last)

        def ln_root_act(act, act_sem, rt_sem, n):
            act.wait_ge(act_sem, n)
            act.activation(stats[:, :, 1], stats[:, :, 1], ACT.Sqrt).then_inc(rt_sem, 1)

        def ln_rows_dve(dve, done):
            with dve.Fori(0, NB) as t:
                dve.tensor_scalar(rows(acc, t), rows(resid, t), stats[:, ds(t, 1), 0], stats[:, ds(t, 1), 1],
                                  ALU.subtract, ALU.mult).then_inc(done, 1)

        def table_view(table):
            return table.rearrange("(t p) d -> p t d", p=P)

        HALF = 8
        TURNS = EC // (2 * HALF)

        def scatter_ring(ctx, tag):
            return dict(idx=sb(ctx, f"{tag}_idx", [P, 2, HALF], i32), rec=sb(ctx, f"{tag}_rec", [P, 2, HALF, 4]),
                        full=new_sem(f"{tag}_full"),
                        sent=[new_sem(f"{tag}_sent{h}") for h in range(2)])

        def scatter_fill(eng, R, i, t, h):
            copy = eng.copy if i == 0 else eng.tensor_copy
            at_least(eng, R["sent"][h], t * 16 * HALF)
            c = t * 2 * HALF + h * HALF
            copy(R["idx"][:, h, :], (pos_src, pos_dst)[i][:, ds(c, HALF)]).then_inc(R["full"], 1)
            copy(R["rec"][:, h, :, :], rec[i][:, ds(c, HALF), :]).then_inc(R["full"], 1)

        def scatter_pool(pool, R, i):
            with pool.Fori(0, TURNS) as t:
                for h in range(2):
                    pool.wait_ge(R["full"], t * 4 + (2 * h + 2))
                    pool.nop(nofuse=True)
                    for j in range(HALF):
                        pool.indirect_dma_start(rec_dram[i][:, :], bass.IndirectOffsetOnAxis(R["idx"][:, h, j:j + 1], 0),
                                                R["rec"][:, h, j, :], None).then_inc(R["sent"][h], 16)
            for h in range(2):
                pool.wait_ge(R["sent"][h], TURNS * 16 * HALF)

        with phase() as ctx:
            sem = lambda n: new_sem(n)
            s_x, s_x2, s_e, s_iota, s_dve, s_edge, s_zero, s_fill, s_pad = (sem(n) for n in (
                "s_x", "s_x2", "s_e", "s_iota", "s_dve", "s_edge", "s_zero", "s_fill", "s_pad"))
            s_var, s_root, s_ln, s_tab = (sem(n) for n in ("s_var", "s_root", "s_ln", "s_tab"))
            ei = [sb(ctx, f"edge_i{i}", [P, EC], i32) for i in range(2)]
            ew = sb(ctx, "edge_w", [P, EC])
            S = rank_scratch(ctx, "edge", EC, ET, wbuf[:, 0:3 * ET])
            key = wbuf[:, 3 * ET:3 * ET + EC]
            tmpi = sb(ctx, "tmpi", [P, ET], i32)
            zeros = wbuf[:, 5 * ET:5 * ET + 2048]
            blank = wbuf[:, 5 * ET + 2048:5 * ET + 2048 + 4 * (ET + 1)]
            st6 = sb(ctx, "st6", [P, NB, 6])
            R = scatter_ring(ctx, "sort0")
            s_sorted = new_sem("s_sorted")
            FILLS = len(rec_dram) + sum(-(-xs.shape[0] * D // P // 2048) for xs in xs_dram)
            block = ctx.enter_context(nc.Block())

            @block.sync
            def _(sp):
                sp.wait_ge(s_pad, 1)
                for buf, arr in ((ei[0], src), (ei[1], dst), (ew, edge_weight)):
                    sp.dma_start(buf[0:EFULL, :], arr[0:EFULL * EC].rearrange("(p c) -> p c", c=EC)).then_inc(s_e, 16)
                    sp.dma_start(buf[EFULL:P, 0:EREST],
                                 arr[EFULL * EC:EDGES].rearrange("(a c) -> a c", a=1)).then_inc(s_e, 16)
                sp.dma_start(resid[:, 0:(NB - 1) * D].rearrange("p (t d) -> p t d", d=D),
                             x[0:(NB - 1) * P, :].rearrange("(t p) d -> p t d", p=P)).then_inc(s_x, 16)
                sp.dma_start(resid[0:TAIL, (NB - 1) * D:], x[(NB - 1) * P:NODES, :]).then_inc(s_x2, 16)
                sp.wait_ge(s_zero, 2)
                for r in rec_dram:
                    sp.dma_start(r.rearrange("(p a) c -> p (a c)", p=P), blank).then_inc(s_fill, 16)
                for xs in xs_dram:
                    n = xs.shape[0] * D // P
                    v = xs.rearrange("(p a) d -> p (a d)", p=P)
                    for a in range(0, n, 2048):
                        sp.dma_start(v[:, a:min(a + 2048, n)], zeros[:, 0:min(2048, n - a)]).then_inc(s_fill, 16)
                sp.wait_ge(s_ln, NB)
                sp.dma_start(table_view(tab[0]), acc[:, 0:NB * D].rearrange("p (t d) -> p t d", d=D))\
                    .then_inc(s_tab, 16)
                sp.wait_ge(s_fill, 16 * FILLS)
                sp.wait_ge(s_tab, 16)

            @block.gpsimd
            def _(pool):
                pool.iota(tmpi[:, :], pattern=[[1, ET]], base=0, channel_multiplier=0).then_inc(s_iota, 1)
                pool.iota(S["ti"][:, 0:1], pattern=[[0, 1]], base=0, channel_multiplier=1).then_inc(s_iota, 1)
                pool.memset(zeros, 0.0).then_inc(s_zero, 1)
                pool.wait_ge(s_fill, 16 * FILLS)
                scatter_pool(pool, R, 0)

            @block.scalar
            def _(act):
                act.wait_ge(s_sorted, 1)
                for h in range(2):
                    scatter_fill(act, R, 0, 0, h)
                with act.Fori(1, TURNS // 2) as t:
                    for h in range(2):
                        scatter_fill(act, R, 0, t, h)
                ln_root_act(act, s_var, s_root, 1)
                with act.Fori(TURNS // 2, TURNS) as t:
                    for h in range(2):
                        scatter_fill(act, R, 0, t, h)

            @block.tensor
            def _(pe):
                rank_pe(pe, NB, ET, S, 1)
                rank_pe(pe, NB, ET, S, 2)

            @block.vector
            def _(dve):
                ch = Chain(dve, s_dve)
                dve.memset(ei[0][:, :], NB * P)
                dve.memset(ei[1][:, :], NB * P)
                dve.memset(ew[:, :], 0.0)
                ch.link(dve.memset(resid[:, (NB - 1) * D:], 0.0))
                dve.sem_inc(s_pad, 1)
                b4 = blank.rearrange("p (a c) -> p a c", c=4)
                ch.link(dve.memset(blank, 0.0))
                dve.memset(b4[:, :, 2], -1.0).then_inc(s_zero, 1)
                dve.memset(ones[:, :], 1.0)
                dve.wait_ge(s_iota, 2)
                dve.tensor_copy(iota_row[:, :], tmpi[:, :])
                ch.link(dve.tensor_copy(iota_col[:, :], S["ti"][:, 0:1]))
                dve.tensor_scalar(ident[:, :], iota_row[:, 0:P], iota_col[:, :], None, ALU.is_equal)
                dve.tensor_scalar(tri_lt[:, :], iota_row[:, 0:P], iota_col[:, :], None, ALU.is_gt)
                ch.link(dve.tensor_scalar(tri_le[:, :], iota_row[:, 0:P], iota_col[:, :], None, ALU.is_ge))
                dve.wait_ge(s_e, 16 * 6)
                for i in range(2):
                    to, frm = ei[i], ei[1 - i]
                    r = rec[i]
                    ch.link(dve.tensor_scalar(r[:, :, 0].bitcast(i32), frm[:, :], float(NODES - 1), None, ALU.min))
                    if i == 0:
                        dve.tensor_copy(r[:, :, 1], ew[:, :])
                    else:
                        dve.memset(r[:, :, 1], 1.0)
                    ch.link(dve.tensor_scalar(tmpi[:, 0:EC], to[:, :], 127, None, ALU.bitwise_and))
                    ch.link(dve.tensor_copy(r[:, :, 2], tmpi[:, 0:EC]))
                    dve.memset(r[:, :, 3], 0.0)
                    ch.link(dve.tensor_scalar(tmpi[:, 0:EC], to[:, :], 7, None, ALU.arith_shift_right))
                    ch.link(dve.tensor_copy(key, tmpi[:, 0:EC]))
                    pos = (pos_src, pos_dst)[i][:, 0:EC]
                    rank_dve(dve, ch, key, EC, NB, ET, pos, edge_map[i], S, iota_row)
                    ch.link(dve.tensor_scalar(tmpi[:, 0:EC], pos, P - 1, None, ALU.bitwise_and))
                    ch.link(dve.tensor_scalar(pos, pos, 7, None, ALU.arith_shift_right))
                    ch.link(dve.scalar_tensor_tensor(pos, tmpi[:, 0:EC], float(ET + 1), pos, ALU.mult, ALU.add))
                    if i == 0:
                        dve.sem_inc(s_sorted, 1)
                dve.wait_ge(s_x, 16)
                dve.wait_ge(s_x2, 16)
                ln_stats_dve(dve, ch, s_var, s_root, st6, 1)
                ln_rows_dve(dve, s_ln)

        def segment_sum(which, table, extra_sp):
            with phase() as ctx:
                tag = f"seg{which}_{table.name}"
                sem = lambda n: new_sem(f"{tag}_{n}")
                recs = sb(ctx, f"{tag}_recs", [P, ET, 4])
                hot = sb(ctx, f"{tag}_hot", [P, UN, P])
                idx = sb(ctx, f"{tag}_idx", [P, 2, 4], i32)
                G = sb(ctx, f"{tag}_G", [P, UN, AW])
                s_rec, s_zero, s_fld, s_hot, s_seg, s_acc = (sem(n) for n in (
                    "rec", "zero", "fld", "hot", "seg", "acc"))
                s_g = [sem(f"g{b}") for b in range(UN)]
                s_w = sem("w")
                block = ctx.enter_context(nc.Block())

                @block.sync
                def _(sp):
                    sp.dma_start(recs[:, :, :], rec_dram[which].rearrange("(p t) c -> p t c", p=P)[:, 0:ET, :])\
                        .then_inc(s_rec, 16)
                    extra_sp(sp, s_w, s_seg)

                @block.gpsimd
                def _(pool):
                    def turn(t):
                        for b in range(UN):
                            if b % 4 == 0:
                                pool.wait_ge(s_fld, t * 2 + (b // 4 + 1))
                            at_least(pool, s_seg, (t - 1) * UN + (b + 1))
                            pool.nop(nofuse=True)
                            pool.indirect_dma_start(G[:, b, 0:D], None, table[:, :],
                                                    bass.IndirectOffsetOnAxis(idx[:, b // 4, b % 4:b % 4 + 1], 0))\
                                .then_inc(s_g[b], 16)

                    turn(0)
                    with pool.Fori(1, ET // UN) as t:
                        turn(t)

                @block.vector
                def _(dve):
                    dve.memset(acc, 0.0).then_inc(s_zero, 1)
                    dve.memset(G[:, :, D:AW], 1.0).then_inc(s_zero, 1)
                    dve.wait_ge(s_zero, 2)
                    dve.wait_ge(s_rec, 16)

                    def one_hot(t, b):
                        at_least(dve, s_seg, (t - 1) * UN + (b + 1))
                        r = ds(t * UN + b, 1)
                        dve.tensor_scalar(hot[:, b, :], iota_row[:, 0:P], recs[:, r, 2], recs[:, r, 1],
                                          ALU.is_equal, ALU.mult).then_inc(s_hot, 1)

                    def add(t, b, blk):
                        dve.wait_ge(s_seg, t * UN + (b + 1))
                        at_least(dve, s_acc, t * UN + b)
                        a = acc[:, ds(blk * AW, AW)]
                        dve.tensor_tensor(a, a, banks[b][:, 0:AW], ALU.add).then_inc(s_acc, 1)

                    def blocks(tile):
                        _, blks = nc.values_load_multi_w_load_instructions(
                            edge_map[which][0:1, ds(tile, UN // 2)], engines=(DVE,), min_val=0, max_val=NB - 1)
                        return blks

                    def turn(t, first=False):
                        if not first:
                            blks = blocks(t * UN - UN // 2)
                        for b in range(UN // 2):
                            one_hot(t, b)
                            if not first:
                                add(t - 1, b + UN // 2, blks[b])
                        blks = blocks(t * UN)
                        for b in range(UN // 2):
                            one_hot(t, b + UN // 2)
                            add(t, b, blks[b])

                    turn(0, True)
                    with dve.Fori(1, ET // UN) as t:
                        turn(t)
                    blks = blocks(ET - UN // 2)
                    for b in range(UN // 2):
                        add(ET // UN - 1, b + UN // 2, blks[b])

                @block.scalar
                def _(act):
                    act.wait_ge(s_rec, 16)

                    def turn(t):
                        for h in range(2):
                            for b in range(4 * h, 4 * h + 4):
                                at_least(act, s_g[b], t * 16)
                            act.copy(idx[:, h, :], recs[:, ds(t * UN + 4 * h, 4), 0].bitcast(i32)).then_inc(s_fld, 1)

                    turn(0)
                    with act.Fori(1, ET // UN) as t:
                        turn(t)

                @block.tensor
                def _(pe):
                    def turn(t):
                        for b in range(UN):
                            pe.wait_ge(s_g[b], t * 16 + 16)
                            pe.wait_ge(s_hot, t * UN + (b + 1))
                            at_least(pe, s_acc, (t - 1) * UN + (b + 1))
                            pe.matmul(banks[b][:, 0:AW], hot[:, b, :], G[:, b, :], start=True, stop=True)\
                                .then_inc(s_seg, 1)

                    pe.wait_ge(s_zero, 2)
                    turn(0)
                    with pe.Fori(1, ET // UN) as t:
                        turn(t)

        def load_experts(m, w, first, last):
            per = MOE[m]["PER"]

            def load(sp, sem, s_seg):
                for e in range(first, last):
                    sp.wait_ge(s_seg, (e + 1) * (ET // (last + 1)))
                    sp.dma_start(wbuf[:, e * per:(e + 1) * per], w[e, :, :]).then_inc(sem, 16)
                sp.wait_ge(sem, 16 * (last - first))
            return load

        HEAD = [ACC0 // m["PER"] for m in MOE]
        segment_sum(0, tab[0], load_experts(0, m1_w, 0, HEAD[0]))

        def moe_route(m, wg, bg, pre_dve, pre_pe, pre_act, pre_sp, pre_sems):
            E, NT = MOE[m]["E"], MOE[m]["NT"]
            with phase() as ctx:
                sem = lambda n: new_sem(f"rt{m}_{n}")
                s_dve, s_var, s_root, s_ln, s_in = (sem(n) for n in ("dve", "var", "root", "ln", "in"))
                s_tp, s_tc, s_gt, s_sc, s_ex, s_exd = (sem(n) for n in ("tp", "tc", "gt", "sc", "ex", "exd"))
                s_slot, s_row, s_st = (sem(n) for n in ("slot", "row", "st"))
                stage = sb(ctx, f"rt{m}_stage", [P, D])
                S = rank_scratch(ctx, f"rt{m}", 2 * NB, NT)
                st6 = sb(ctx, f"rt{m}_st6", [P, NB, 6])
                wg_sb = sb(ctx, f"rt{m}_wg", [P, 2, E])
                bg_sb = sb(ctx, f"rt{m}_bg", [P, E])
                xT = sb(ctx, f"rt{m}_xT", [P, 2, P])
                score = sb(ctx, f"rt{m}_score", [P, NB, E])
                top8 = sb(ctx, f"rt{m}_top8", [P, NB, 8])
                ind8 = sb(ctx, f"rt{m}_ind8", [P, NB, 8], mybir.dt.uint32)
                keyf = sb(ctx, f"rt{m}_key", [P, NB, 2])
                key2 = keyf[:, :, :].rearrange("p t s -> p (t s)")
                valid = sb(ctx, f"rt{m}_valid", [P, 2])
                pre = pre_sems(ctx)
                block = ctx.enter_context(nc.Block())

                @block.sync
                def _(sp):
                    sp.dma_start(wg_sb[:, :, :], wg).then_inc(s_in, 16)
                    sp.dma_start(bg_sb[:, :], bg.partition_broadcast(P)).then_inc(s_in, 16)
                    pre_sp(sp, pre)
                    sp.wait_ge(s_in, 32)

                @block.scalar
                def _(act):
                    pre_act(act, pre, stage)
                    ln_root_act(act, s_var, s_root, 1)

                    def turn(t):
                        act.wait_ge(s_ln, t + 1)
                        at_least(act, s_tp, t)
                        act.copy(stage[:, :], rows(acc, t)).then_inc(s_st, 1)

                    turn(0)
                    with act.Fori(1, NB) as t:
                        turn(t)
                    act.wait_ge(s_ex, 1)
                    act.activation(prob[:, 1, :], prob[:, 1, :], ACT.Exp).then_inc(s_exd, 1)

                @block.tensor
                def _(pe):
                    pre_pe(pe, pre, stage)
                    pe.wait_ge(s_in, 32)

                    def turn(t):
                        pe.wait_ge(s_st, t + 1)
                        at_least(pe, s_tc, t)
                        for k in range(2):
                            mm = pe.transpose(banks[5][:, k * P:(k + 1) * P], stage[:, k * P:(k + 1) * P], ident[:, :])
                        mm.then_inc(s_tp, 1)
                        pe.wait_ge(s_tc, t + 1)
                        at_least(pe, s_sc, t)
                        for k in range(2):
                            mm = pe.matmul(banks[6][:, 0:E], xT[:, k, :], wg_sb[:, k, :], start=(k == 0), stop=(k == 1))
                        mm.then_inc(s_gt, 1)

                    turn(0)
                    with pe.Fori(1, NB) as t:
                        turn(t)
                    rank_pe(pe, E, NT, S, 1)

                @block.vector
                def _(dve):
                    ch = Chain(dve, s_dve)
                    pre_dve(dve, ch, pre)
                    ln_stats_dve(dve, ch, s_var, s_root, st6, 1)
                    ln_rows_dve(dve, s_ln)
                    dve.wait_ge(s_in, 32)

                    def turn(t):
                        dve.wait_ge(s_tp, t + 1)
                        at_least(dve, s_gt, t)
                        dve.tensor_copy(xT[:, :, :].rearrange("p k n -> p (k n)"), banks[5][:, 0:2 * P]).then_inc(s_tc, 1)
                        dve.wait_ge(s_gt, t + 1)
                        dve.tensor_tensor(score[:, ds(t, 1), :].rearrange("p a e -> p (a e)"), banks[6][:, 0:E],
                                          bg_sb[:, :], ALU.add).then_inc(s_sc, 1)

                    turn(0)
                    with dve.Fori(1, NB) as t:
                        turn(t)
                    dve.wait_ge(s_sc, NB)
                    for t in range(NB):
                        last = dve.max(top8[:, t, :], score[:, t, :])
                    ch.link(last)
                    for t in range(NB):
                        last = dve.max_index(ind8[:, t, :], top8[:, t, :], score[:, t, :])
                    ch.link(last)
                    dve.tensor_tensor(prob[:, 1, :], top8[:, :, 1], top8[:, :, 0], ALU.subtract).then_inc(s_ex, 1)
                    dve.wait_ge(s_exd, 1)
                    ch.link(dve.tensor_scalar(prob[:, 0, :], prob[:, 1, :], 1.0, None, ALU.add))
                    ch.link(dve.reciprocal(prob[:, 0, :], prob[:, 0, :]))
                    ch.link(dve.tensor_tensor(prob[:, 1, :], prob[:, 1, :], prob[:, 0, :], ALU.mult))
                    ch.link(dve.tensor_copy(keyf[:, :, :], ind8[:, :, 0:2]))
                    ch.link(dve.tensor_scalar(valid[:, 0:1], iota_col[:, :], float(TAIL), None, ALU.is_ge))
                    ch.link(dve.tensor_scalar(valid[:, 0:1], valid[:, 0:1], float(E), None, ALU.mult))
                    ch.link(dve.tensor_scalar(keyf[:, NB - 1, :], keyf[:, NB - 1, :], valid[:, 0:1], None, ALU.max))
                    rank_dve(dve, ch, key2, 2 * NB, E, NT, slot[:, :], exp_map[m], S, iota_row)
                    dve.sem_inc(s_slot, 1)

                @block.gpsimd
                def _(pool):
                    pool.wait_ge(s_slot, 1)
                    for j in range(2 * NB):
                        pool.indirect_dma_start(xs_dram[m][:, :], bass.IndirectOffsetOnAxis(slot[:, j:j + 1], 0),
                                                acc[:, j // 2 * D:(j // 2 + 1) * D], None).then_inc(s_row, 16)
                    pool.wait_ge(s_row, 2 * NB * 16)

        def moe_experts(m, load, sort):
            E, H, NT, PER = (MOE[m][k] for k in ("E", "H", "NT", "PER"))
            NH, NJ = H // 512, H // P
            NG = NJ // 4
            hb, tb, yb, xb = banks[0:NH], banks[2:2 + NG], banks[4], banks[5]
            with phase() as ctx:
                sem = lambda n: new_sem(f"ff{m}_{n}")
                s_w, s_tx, s_xt, s_up, s_h, s_th, s_ht, s_dn, s_y = (sem(n) for n in (
                    "w", "tx", "xt", "up", "h", "th", "ht", "dn", "y"))
                s_xs, s_st = ([sem(f"{n}{b}") for b in range(2)] for n in ("xs", "st"))
                xs = sb(ctx, f"ff{m}_xs", [P, 2, D])
                xT = sb(ctx, f"ff{m}_xT", [P, 2, P])
                h = sb(ctx, f"ff{m}_h", [P, H])
                hT = sb(ctx, f"ff{m}_hT", [P, NJ, P])
                y = sb(ctx, f"ff{m}_y", [P, 2, D])
                b1_sb = sb(ctx, f"ff{m}_b1", [P, E * NJ])
                b2_sb = sb(ctx, f"ff{m}_b2", [P, E * D])
                R = scatter_ring(ctx, "sort1") if sort else None
                block = ctx.enter_context(nc.Block())

                def pairs(eng, body):
                    body(0, True)
                    n = TURNS if sort else NT // 2
                    with eng.Fori(1, n) as u:
                        body(u, True)
                    if n < NT // 2:
                        with eng.Fori(n, NT // 2) as u:
                            body(u, False)

                @block.sync
                def _(sp):
                    n_w = load(sp, s_w, b1_sb, b2_sb)
                    assert n_w == MOE_LOADS[m]

                    def fetch(u, b):
                        at_least(sp, s_tx, u * 2 + (b - 1))
                        sp.dma_start(xs[:, b, :], xs_dram[m][ds((u * 2 + b) * P, P), :]).then_inc(s_xs[b], 16)

                    def store(u, b):
                        sp.wait_ge(s_y, u * 2 + (b + 1))
                        sp.dma_start(ys_dram[m][ds((u * 2 + b) * P, P), :], y[:, b, :]).then_inc(s_st[b], 16)

                    fetch(0, 0)
                    fetch(0, 1)

                    def body(u, first):
                        fetch(u + 1, 0)
                        if not isinstance(u, int):
                            store(u - 1, 1)
                        fetch(u + 1, 1)
                        store(u, 0)

                    pairs(sp, body)
                    store(NT // 2 - 1, 1)
                    for b in range(2):
                        sp.wait_ge(s_xs[b], 16 * (NT // 2 + 1))
                        sp.wait_ge(s_st[b], 16 * (NT // 2))

                @block.tensor
                def _(pe):
                    def turn_x(t, u, b):
                        pe.wait_ge(s_xs[b], u * 16 + 16)
                        at_least(pe, s_xt, t)
                        for k in range(2):
                            mm = pe.transpose(xb[:, k * P:(k + 1) * P], xs[:, b, k * P:(k + 1) * P], ident[:, :])
                        mm.then_inc(s_tx, 1)

                    def up(t, e):
                        pe.wait_ge(s_xt, t + 1)
                        at_least(pe, s_h, t * NH)
                        for n in range(NH):
                            for k in range(2):
                                mm = pe.matmul(hb[n][:, :], xT[:, k, :],
                                               wbuf[:, ds(e * PER + (k * H + n * 512), 512)],
                                               start=(k == 0), stop=(k == 1))
                            mm.then_inc(s_up, 1)

                    def turn_h(t):
                        pe.wait_ge(s_h, t * NH + NH)
                        at_least(pe, s_ht, t * NG)
                        for g in range(NG):
                            for j in range(4):
                                mm = pe.transpose(tb[g][:, j * P:(j + 1) * P],
                                                  h[:, (4 * g + j) * P:(4 * g + j + 1) * P], ident[:, :])
                            mm.then_inc(s_th, 1)

                    def down(t, e):
                        pe.wait_ge(s_ht, t * NG + NG)
                        at_least(pe, s_y, t)
                        for j in range(NJ):
                            mm = pe.matmul(yb[:, 0:D], hT[:, j, :], wbuf[:, ds(e * PER + (2 * H + j * D), D)],
                                           start=(j == 0), stop=(j == NJ - 1))
                        mm.then_inc(s_dn, 1)

                    def expert(t):
                        return pe.value_load(exp_map[m][0:1, ds(t, 1)], min_val=0, max_val=E - 1)

                    pe.wait_ge(s_w, MOE_LOADS[m] * 16)
                    turn_x(0, 0, 0)

                    def body(u, first):
                        for b in range(2):
                            t = u * 2 + b
                            up(t, expert(t))
                            turn_x(t + 1, u + b, 1 - b)
                            if not (isinstance(t, int) and t == 0):
                                down(t - 1, expert(t - 1))
                            turn_h(t)

                    pairs(pe, body)
                    down(NT - 1, expert(NT - 1))

                @block.scalar
                def _(act):
                    act.wait_ge(s_w, MOE_LOADS[m] * 16)

                    def turn(t):
                        e = act.value_load(exp_map[m][0:1, ds(t, 1)], min_val=0, max_val=E - 1)
                        for g in range(NG):
                            act.wait_ge(s_th, t * NG + (g + 1))
                            at_least(act, s_dn, t)
                            for j in range(4):
                                q = 4 * g + j
                                last = act.activation(hT[:, q, :], tb[g][:, j * P:(j + 1) * P], ACT.Relu,
                                                      bias=b1_sb[:, ds(e * NJ + q, 1)])
                            last.then_inc(s_ht, 1)

                    turn(0)
                    with act.Fori(1, NT) as t:
                        turn(t)

                @block.vector
                def _(dve):
                    dve.wait_ge(s_w, MOE_LOADS[m] * 16)

                    def copy_x(t):
                        dve.wait_ge(s_tx, t + 1)
                        at_least(dve, s_up, t * NH)
                        dve.tensor_copy(xT[:, :, :].rearrange("p k n -> p (k n)"), xb[:, 0:2 * P]).then_inc(s_xt, 1)

                    def copy_h(t):
                        at_least(dve, s_th, t * NG)
                        for n in range(NH):
                            dve.wait_ge(s_up, t * NH + (n + 1))
                            dve.tensor_copy(h[:, n * 512:(n + 1) * 512], hb[n][:, :]).then_inc(s_h, 1)

                    def copy_y(t, u, b):
                        e = dve.value_load(exp_map[m][0:1, ds(t, 1)], min_val=0, max_val=E - 1)
                        dve.wait_ge(s_dn, t + 1)
                        at_least(dve, s_st[b], u * 16)
                        dve.tensor_tensor(y[:, b, :], yb[:, 0:D], b2_sb[:, ds(e * D, D)], ALU.add).then_inc(s_y, 1)

                    copy_x(0)

                    def body(u, first):
                        for b in range(2):
                            t = u * 2 + b
                            copy_h(t)
                            copy_x(t + 1)
                            if not (isinstance(t, int) and t == 0):
                                copy_y(t - 1, u - 1 + b, 1 - b)
                            if sort and first:
                                scatter_fill(dve, R, 1, u, b)

                    pairs(dve, body)
                    copy_y(NT - 1, NT // 2 - 1, 1)

                if sort:
                    @block.gpsimd
                    def _(pool):
                        scatter_pool(pool, R, 1)

        def moe_combine(m, post_dve, post_act, post_sp, post_sems):
            target = resid if m == 0 else acc
            with phase() as ctx:
                sem = lambda n: new_sem(f"cb{m}_{n}")
                s_idx, s_use, s_add, s_dve, s_pre = (sem(n) for n in ("idx", "use", "add", "dve", "pre"))
                s_g = [sem(f"g{j}") for j in range(2 * RG)]
                Y = sb(ctx, f"cb{m}_Y", [P, 2 * RG, D])
                idx = sb(ctx, f"cb{m}_idx", [P, 2 * NB], i32)
                post = post_sems(ctx)
                block = ctx.enter_context(nc.Block())

                @block.gpsimd
                def _(pool):
                    for j in range(2 * NB):
                        b = j % (2 * RG)
                        if j >= 2 * RG:
                            pool.wait_ge(s_add, j - 2 * RG + 1)
                        if j == 0:
                            pool.wait_ge(s_idx, 1)
                        pool.indirect_dma_start(Y[:, b, :], None, ys_dram[m][:, :],
                                                bass.IndirectOffsetOnAxis(idx[:, j:j + 1], 0)).then_inc(s_g[b], 16)

                @block.vector
                def _(dve):
                    ch = Chain(dve, s_dve)
                    dve.tensor_scalar(idx[:, :], slot[:, :], float(MOE[m]["NT"] * P - 1), None, ALU.min)\
                        .then_inc(s_idx, 1)
                    if m == 1:
                        ln_rows_dve(dve, s_pre)
                        dve.wait_ge(s_pre, NB)

                    def turn(t):
                        for j in range(2 * RG):
                            dve.wait_ge(s_g[j], t * 16 + 16)
                            r = target[:, ds((t * RG + j // 2) * D, D)]
                            if j % 2:
                                dve.wait_ge(s_add, t * 2 * RG + j)
                            dve.scalar_tensor_tensor(r, Y[:, j, :], prob[:, j % 2, ds(t * RG + j // 2, 1)], r,
                                                     ALU.mult, ALU.add).then_inc(s_add, 1)

                    turn(0)
                    with dve.Fori(1, NB // RG) as t:
                        turn(t)
                    dve.wait_ge(s_add, 2 * NB)
                    post_dve(dve, ch, post)

                @block.scalar
                def _(act):
                    post_act(act, post)

                @block.sync
                def _(sp):
                    post_sp(sp, post)

        def pre0_sems(ctx):
            p = {k: new_sem(f"l0_{k}") for k in ("w", "st", "tp", "tc", "mm", "up")}
            p["W"] = sb(ctx, "l0_W", [P, 2, D])
            p["B"] = sb(ctx, "l0_B", [P, D])
            p["T"] = sb(ctx, "l0_T", [P, 2, P])
            return p

        def pre0_sp(sp, p):
            sp.dma_start(p["W"][:, :, :], l0_w).then_inc(p["w"], 16)
            sp.dma_start(p["B"][:, :], l0_b.partition_broadcast(P)).then_inc(p["w"], 16)

        def pre0_act(act, p, stage):
            def turn(t):
                at_least(act, p["tp"], t)
                act.copy(stage[:, :], acc[:, ds(t * AW, D)]).then_inc(p["st"], 1)

            turn(0)
            with act.Fori(1, NB) as t:
                turn(t)
            act.wait_ge(p["tp"], NB)

        def pre0_pe(pe, p, stage):
            pe.wait_ge(p["w"], 32)

            def turn(t):
                pe.wait_ge(p["st"], t + 1)
                at_least(pe, p["tc"], t)
                for k in range(2):
                    mm = pe.transpose(banks[0][:, k * P:(k + 1) * P], stage[:, k * P:(k + 1) * P], ident[:, :])
                mm.then_inc(p["tp"], 1)
                pe.wait_ge(p["tc"], t + 1)
                at_least(pe, p["up"], t)
                for k in range(2):
                    mm = pe.matmul(banks[1][:, 0:D], p["T"][:, k, :], p["W"][:, k, :], start=(k == 0), stop=(k == 1))
                mm.then_inc(p["mm"], 1)

            turn(0)
            with pe.Fori(1, NB) as t:
                turn(t)

        def pre0_dve(dve, ch, p):
            dve.wait_ge(p["w"], 32)

            def turn(t):
                dve.wait_ge(p["tp"], t + 1)
                at_least(dve, p["mm"], t)
                dve.tensor_copy(p["T"][:, :, :].rearrange("p k n -> p (k n)"), banks[0][:, 0:2 * P]).then_inc(p["tc"], 1)
                ch.link(dve.tensor_tensor(rows(resid, t), rows(resid, t), p["B"][:, :], ALU.add))
                dve.wait_ge(p["mm"], t + 1)
                dve.tensor_tensor(rows(resid, t), rows(resid, t), banks[1][:, 0:D], ALU.add).then_inc(p["up"], 1)

            ch.loop(0, 1)
            turn(0)
            ch.leave(1)
            with dve.Fori(1, NB) as t:
                ch.loop(t - 1, 1)
                turn(t)
            ch.leave(NB - 1)
            dve.wait_ge(p["up"], NB)

        moe_route(0, m1_wg, m1_bg, pre0_dve, pre0_pe, pre0_act, pre0_sp, pre0_sems)

        MOE_LOADS = [m["E"] - head + 2 for m, head in zip(MOE, HEAD)]

        def load_rest(m, w, b1, b2):
            def load(sp, sem, b1_sb, b2_sb):
                per = MOE[m]["PER"]
                for e in range(HEAD[m], MOE[m]["E"]):
                    sp.dma_start(wbuf[:, e * per:(e + 1) * per], w[e, :, :]).then_inc(sem, 16)
                sp.dma_start(b1_sb[:, :], b1).then_inc(sem, 16)
                sp.dma_start(b2_sb[:, :], b2.partition_broadcast(P)).then_inc(sem, 16)
                return MOE[m]["E"] - HEAD[m] + 2
            return load

        moe_experts(0, load_rest(0, m1_w, m1_b1, m1_b2), True)

        def post0_sems(ctx):
            p = {k: new_sem(f"post0_{k}") for k in ("var", "root", "ln", "tab")}
            p["st6"] = sb(ctx, "post0_st6", [P, NB, 6])
            return p

        def post0_dve(dve, ch, p):
            ln_stats_dve(dve, ch, p["var"], p["root"], p["st6"], 1)
            ln_rows_dve(dve, p["ln"])

        def post0_act(act, p):
            ln_root_act(act, p["var"], p["root"], 1)

        def post0_sp(sp, p):
            sp.wait_ge(p["ln"], NB)
            sp.dma_start(table_view(tab[1]), acc[:, 0:NB * D].rearrange("p (t d) -> p t d", d=D)).then_inc(p["tab"], 16)
            sp.wait_ge(p["tab"], 16)

        moe_combine(0, post0_dve, post0_act, post0_sp, post0_sems)

        segment_sum(1, tab[1], load_experts(1, m2_w, 0, HEAD[1]))

        with phase() as ctx:
            sem = lambda n: new_sem(f"sage_{n}")
            s_w, s_dve, s_in, s_tp, s_tc, s_m1, s_h, s_th, s_ht, s_m2, s_z, s_st = (sem(n) for n in (
                "w", "dve", "in", "tp", "tc", "m1", "h", "th", "ht", "m2", "z", "st"))
            W1 = sb(ctx, "sage_W1", [P, 4, HID])
            W2 = sb(ctx, "sage_W2", [P, 4, 2 * D])
            B1 = sb(ctx, "sage_B1", [P, HID])
            B2 = sb(ctx, "sage_B2", [P, D])
            mx = sb(ctx, "sage_mx", [P, 2, D])
            mxT = sb(ctx, "sage_mxT", [P, 4, P])
            h = sb(ctx, "sage_h", [P, HID])
            hT = sb(ctx, "sage_hT", [P, 4, P])
            z = sb(ctx, "sage_z", [P, D])
            accv = acc.rearrange("p (t a) -> p t a", a=AW)
            block = ctx.enter_context(nc.Block())

            @block.sync
            def _(sp):
                sp.dma_start(W1[:, 0:2, :], g_w1l).then_inc(s_w, 16)
                sp.dma_start(W1[:, 2:4, :], g_w1r).then_inc(s_w, 16)
                sp.dma_start(W2[:, :, :], g_w2).then_inc(s_w, 16)
                sp.dma_start(B1[:, :], g_b1l.partition_broadcast(P)).then_inc(s_w, 16)
                sp.dma_start(B2[:, :], g_b2l.partition_broadcast(P)).then_inc(s_w, 16)
                with sp.Fori(0, NB) as t:
                    sp.wait_ge(s_z, t * 2 + 1)
                    sp.dma_start(tab[2][ds(t * P, P), :], z[:, :]).then_inc(s_st, 16)
                sp.wait_ge(s_st, NB * 16)

            @block.tensor
            def _(pe):
                pe.wait_ge(s_w, 80)

                def turn_rows(t):
                    pe.wait_ge(s_in, t * 2 + 2)
                    at_least(pe, s_tc, t)
                    for q in range(4):
                        mm = pe.transpose(banks[0][:, q * P:(q + 1) * P],
                                          mx[:, q // 2, (q % 2) * P:(q % 2 + 1) * P], ident[:, :])
                    mm.then_inc(s_tp, 1)

                def first_layer(t):
                    pe.wait_ge(s_tc, t + 1)
                    at_least(pe, s_h, t)
                    for q in range(4):
                        mm = pe.matmul(banks[1][:, :], mxT[:, q, :], W1[:, q, :], start=(q == 0), stop=(q == 3))
                    mm.then_inc(s_m1, 1)

                def turn_hidden(t):
                    pe.wait_ge(s_h, t + 1)
                    at_least(pe, s_ht, t)
                    for q in range(4):
                        mm = pe.transpose(banks[2][:, q * P:(q + 1) * P], h[:, q * P:(q + 1) * P], ident[:, :])
                    mm.then_inc(s_th, 1)

                def second_layer(t):
                    pe.wait_ge(s_ht, t + 1)
                    at_least(pe, s_z, t * 2)
                    for q in range(4):
                        mm = pe.matmul(banks[3][:, :], hT[:, q, :], W2[:, q, :], start=(q == 0), stop=(q == 3))
                    mm.then_inc(s_m2, 1)

                turn_rows(0)
                first_layer(0)
                turn_rows(1)
                turn_hidden(0)
                with pe.Fori(1, NB - 1) as t:
                    first_layer(t)
                    turn_rows(t + 1)
                    second_layer(t - 1)
                    turn_hidden(t)
                first_layer(NB - 1)
                second_layer(NB - 2)
                turn_hidden(NB - 1)
                second_layer(NB - 1)

            @block.scalar
            def _(act):
                def copy_rows(t):
                    act.wait_ge(s_tp, t + 1)
                    at_least(act, s_m1, t)
                    act.activation(mxT[:, :, :].rearrange("p k n -> p (k n)"), banks[0][:, :], ACT.Copy).then_inc(s_tc, 1)

                def relu(t):
                    act.wait_ge(s_th, t + 1)
                    at_least(act, s_m2, t)
                    act.activation(hT[:, :, :].rearrange("p k n -> p (k n)"), banks[2][:, :], ACT.Relu).then_inc(s_ht, 1)

                copy_rows(0)
                copy_rows(1)
                relu(0)
                with act.Fori(1, NB - 1) as t:
                    copy_rows(t + 1)
                    relu(t)
                relu(NB - 1)

            @block.vector
            def _(dve):
                ch = Chain(dve, s_dve)
                dve.wait_ge(s_w, 80)
                ch.link(dve.tensor_scalar(inv_cnt[:, :], accv[:, :, D], 1.0, None, ALU.max))
                ch.link(dve.reciprocal(inv_cnt[:, :], inv_cnt[:, :]))

                def rows_in(t):
                    at_least(dve, s_tp, t)
                    dve.tensor_scalar(mx[:, 0, :], acc[:, ds(t * AW, D)], inv_cnt[:, ds(t, 1)], None, ALU.mult)\
                        .then_inc(s_in, 1)
                    dve.tensor_scalar(mx[:, 1, :], rows(resid, t), stats[:, ds(t, 1), 0], stats[:, ds(t, 1), 1],
                                      ALU.subtract, ALU.mult).then_inc(s_in, 1)

                def hidden(t):
                    dve.wait_ge(s_m1, t + 1)
                    at_least(dve, s_th, t)
                    dve.tensor_tensor(h[:, :], banks[1][:, :], B1[:, :], ALU.add).then_inc(s_h, 1)

                def results(t):
                    ch.link(dve.tensor_tensor(rows(resid, t), rows(resid, t), B2[:, :], ALU.add))
                    dve.wait_ge(s_m2, t + 1)
                    at_least(dve, s_st, t * 16)
                    dve.tensor_copy(z[:, :], banks[3][:, 0:D]).then_inc(s_z, 1)
                    dve.tensor_tensor(rows(resid, t), rows(resid, t), banks[3][:, D:2 * D], ALU.add).then_inc(s_z, 1)

                rows_in(0)
                rows_in(1)
                hidden(0)
                dve.wait_ge(s_in, 4)
                with dve.Fori(1, NB - 1) as t:
                    ch.loop(t - 1, 1)
                    hidden(t)
                    rows_in(t + 1)
                    results(t - 1)
                ch.leave(NB - 2)
                hidden(NB - 1)
                results(NB - 2)
                dve.wait_ge(s_in, 2 * NB)
                results(NB - 1)

        segment_sum(1, tab[2], lambda sp, sem, s_seg: None)

        def pre1_sems(ctx):
            return dict(up=new_sem("pre1_up"))

        def pre1_dve(dve, ch, p):
            with dve.Fori(0, NB) as t:
                dve.scalar_tensor_tensor(rows(resid, t), acc[:, ds(t * AW, D)], inv_cnt[:, ds(t, 1)],
                                         rows(resid, t), ALU.mult, ALU.add).then_inc(p["up"], 1)
            dve.wait_ge(p["up"], NB)

        moe_route(1, m2_wg, m2_bg, pre1_dve, lambda pe, p, s: None, lambda act, p, s: None, lambda sp, p: None, pre1_sems)

        moe_experts(1, load_rest(1, m2_w, m2_b1, m2_b2), False)

        def post1_sems(ctx):
            p = {k: new_sem(f"post1_{k}") for k in ("w", "var", "root", "up", "out")}
            p["st6"] = sb(ctx, "post1_st6", [P, NB, 6])
            p["G"] = sb(ctx, "post1_G", [P, D])
            p["B"] = sb(ctx, "post1_B", [P, D])
            return p

        def post1_dve(dve, ch, p):
            rows_stats(dve, ch, acc, p["st6"])
            dve.tensor_scalar(stats[:, :, 1], stats[:, :, 1], EPS, None, ALU.add).then_inc(p["var"], 1)
            dve.wait_ge(p["root"], 1)
            ch.link(dve.reciprocal(stats[:, :, 1], stats[:, :, 1]))
            dve.wait_ge(p["w"], 32)
            with dve.Fori(0, NB) as t:
                ch.loop(t, 3)
                a = rows(acc, t)
                ch.link(dve.tensor_scalar(a, a, stats[:, ds(t, 1), 0], stats[:, ds(t, 1), 1],
                                          ALU.subtract, ALU.mult))
                ch.link(dve.tensor_tensor(a, a, p["G"][:, :], ALU.mult))
                ch.link(dve.tensor_tensor(a, a, p["B"][:, :], ALU.add))
                dve.tensor_tensor(rows(resid, t), rows(resid, t), a, ALU.add).then_inc(p["up"], 1)
            ch.leave(NB)

        def post1_act(act, p):
            ln_root_act(act, p["var"], p["root"], 1)

        def post1_sp(sp, p):
            sp.dma_start(p["G"][:, :], gamma.partition_broadcast(P)).then_inc(p["w"], 16)
            sp.dma_start(p["B"][:, :], beta.partition_broadcast(P)).then_inc(p["w"], 16)
            with sp.Fori(0, NB - 1) as t:
                sp.wait_ge(p["up"], t + 1)
                sp.dma_start(out[ds(t * P, P), :], rows(resid, t)).then_inc(p["out"], 16)
            sp.wait_ge(p["up"], NB)
            sp.dma_start(out[(NB - 1) * P:NODES, :], resid[0:TAIL, (NB - 1) * D:]).then_inc(p["out"], 16)
            sp.wait_ge(p["out"], NB * 16)

        moe_combine(1, post1_dve, post1_act, post1_sp, post1_sems)


def kernel(**inputs):
    import numpy as _np
    import concourse.bacc as _bacc
    from concourse import mybir as _mybir
    from concourse.bass_utils import run_bass_kernel_spmd as _run

    def up(a, *order):
        a = _np.transpose(_np.asarray(a), order) if order else _np.asarray(a)
        return a.reshape(a.shape[0] // 128, 128, -1).transpose(1, 0, 2)

    def experts(w_up, w_down):
        parts = [w.reshape(w.shape[0], w.shape[1] // 128, 128, -1).transpose(0, 2, 1, 3).reshape(w.shape[0], 128, -1)
                 for w in (w_up, w_down)]
        return _np.concatenate(parts, axis=2)

    g = {k: _np.asarray(v) for k, v in inputs.items()}
    args = dict(
        x=g["x"], src=g["src"], dst=g["dst"], edge_weight=g["edge_weight"],
        l0_w=up(g["L0_gnn_W"], 1, 0), l0_b=g["L0_gnn_b"],
        m1_wg=up(g["L0_ffn_Wg"], 1, 0), m1_bg=g["L0_ffn_bg"],
        m1_w=experts(g["L0_ffn_W1"].transpose(0, 2, 1), g["L0_ffn_W2"].transpose(0, 2, 1)),
        m1_b1=g["L0_ffn_b1"].reshape(8 * 8, 128).T, m1_b2=g["L0_ffn_b2"].reshape(-1),
        g_w1l=up(g["L1_gnn_W1l"], 1, 0), g_b1l=g["L1_gnn_b1l"], g_w1r=up(g["L1_gnn_W1r"], 1, 0),
        g_w2=_np.concatenate([up(g["L1_gnn_W2l"], 1, 0), up(g["L1_gnn_W2r"], 1, 0)], axis=2),
        g_b2l=g["L1_gnn_b2l"],
        m2_wg=up(g["L1_ffn_gate_w"]), m2_bg=g["L1_ffn_gate_b"], m2_w=experts(g["L1_ffn_w1"], g["L1_ffn_w2"]),
        m2_b1=g["L1_ffn_b1"].reshape(16 * 4, 128).T, m2_b2=g["L1_ffn_b2"].reshape(-1),
        gamma=g["L1_ffn_gamma"], beta=g["L1_ffn_beta"])
    nc = _bacc.Bacc("TRN2", target_bir_lowering=False, num_devices=1)
    arrays, aps = {}, {}
    for name, a in args.items():
        a = _np.ascontiguousarray(a)
        arrays[f"in_{name}"] = a
        aps[name] = nc.dram_tensor(f"in_{name}", a.shape, _mybir.dt.from_np(a.dtype), kind="ExternalInput").ap()
    aps["out"] = nc.dram_tensor("out_0", (3125, 256), _mybir.dt.float32, kind="ExternalOutput").ap()
    gnn_moe_program(nc, **aps)
    r = _run(nc, [arrays], core_ids=[0])
    return r.results[0]["out_0"]
```

```python
import concourse.bass as bass
from concourse import mybir
from contextlib import ExitStack, contextmanager


P = 128
NODES = 3125
EDGES = 53125
D = 256
NB = -(-NODES // P)
TAIL = NODES - (NB - 1) * P
EC = -(-EDGES // P)
EFULL = EDGES // EC
EREST = EDGES - EFULL * EC
UN = 8
ET = -(-((EDGES + NB * (P - 1)) // P) // UN) * UN
HID = 512
AW = D + 2
EPS = 1e-5
MOE = (dict(E=8, H=1024), dict(E=16, H=512))
for _m in MOE:
    _m["NT"] = (2 * NODES + _m["E"] * (P - 1)) // P
    _m["PER"] = 2 * D * _m["H"] // P
WB = MOE[0]["E"] * MOE[0]["PER"]
ACC0 = WB - NB * AW
PCOL = 64
PARTS = 6
RG = 5


def at_least(eng, sem, value):
    if isinstance(value, int) and value <= 0:
        return
    eng.wait_ge(sem, value)


class Chain:

    def __init__(self, eng, sem):
        self.eng, self.sem, self.base, self.n = eng, sem, 0, 0

    def link(self, ins):
        ins.then_inc(self.sem, 1)
        self.n += 1
        self.eng.wait_ge(self.sem, self.base + self.n)

    def loop(self, turn, steps):
        self.outer = self.base + self.n
        self.base, self.n, self.steps = turn * steps + self.outer, 0, steps

    def leave(self, turns):
        assert self.n == self.steps, (self.n, self.steps)
        self.base, self.n = self.outer + turns * self.steps, 0


def gnn_moe_program(nc, x, src, dst, edge_weight, l0_w, l0_b, m1_wg, m1_bg, m1_w, m1_b1, m1_b2,
                    g_w1l, g_b1l, g_w1r, g_w2, g_b2l, m2_wg, m2_bg, m2_w, m2_b1, m2_b2, gamma, beta, out):
    f32, i32 = mybir.dt.float32, mybir.dt.int32
    bf16, f16 = mybir.dt.bfloat16, mybir.dt.float16
    ALU, ACT = mybir.AluOpType, mybir.ActivationFunctionType
    ds = bass.ds
    DVE = mybir.EngineType.DVE

    top = ExitStack()
    with top:
        def sb(ctx, name, shape, dt=f32):
            return ctx.enter_context(nc.sbuf_tensor(name, shape, dt))

        open_sems = []

        def new_sem(name):
            open_sems.append(nc.alloc_semaphore(name))
            return open_sems[-1]

        @contextmanager
        def phase():
            with ExitStack() as ctx:
                yield ctx
            nc.clear_and_free_semaphores(open_sems)
            nc.all_engine_barrier()
            open_sems.clear()

        tab = [nc.dram_tensor(f"table{i}", (NB * P, D), f32).ap() for i in range(3)]
        rec_dram = [nc.dram_tensor(f"records{i}", ((ET + 1) * P, 4), f32).ap() for i in range(2)]
        xs_dram = [nc.dram_tensor(f"slots_x{i}", ((m["NT"] + 2) * P, D), f32).ap() for i, m in enumerate(MOE)]
        ys_dram = [nc.dram_tensor(f"slots_y{i}", (m["NT"] * P, D), f32).ap() for i, m in enumerate(MOE)]

        wbuf = sb(top, "wbuf", [P, WB])
        acc = wbuf[:, ACC0:WB]
        resid = sb(top, "resid", [P, NB * D])
        ident = sb(top, "ident", [P, P])
        tri_lt = sb(top, "tri_lt", [P, P])
        tri_le = sb(top, "tri_le", [P, P])
        iota_row = sb(top, "iota_row", [P, ET])
        iota_col = sb(top, "iota_col", [P, 1])
        ones = sb(top, "ones", [P, EC])
        stats = sb(top, "stats", [P, NB, 2])
        inv_cnt = sb(top, "inv_cnt", [P, NB])
        edge_map = [sb(top, f"edge_map{i}", [1, ET], i32) for i in range(2)]
        exp_map = [sb(top, f"exp_map{i}", [1, m["NT"]], i32) for i, m in enumerate(MOE)]
        pos_src = wbuf[:, 12288:12288 + EC].bitcast(i32)
        pos_dst = sb(top, "pos_dst", [P, EC], i32)
        rec = [wbuf[:, 10240:10240 + 4 * EC].rearrange("p (c f) -> p c f", f=4),
               sb(top, "rec1", [P, EC, 4])]
        slot = sb(top, "slot", [P, 2 * NB], i32)
        prob = sb(top, "prob", [P, 2, NB])

        banks = [top.enter_context(nc.psum_tensor(f"bank{i}", [P, 512], f32)) for i in range(8)]

        def rows(tile_ap, t, width=D):
            return tile_ap[:, ds(t * width, width)]

        def groups(eng, ahead, behind):
            def turn(t, last):
                for b in range(RG):
                    if b < RG - 1:
                        ahead(t, b + 1)
                    elif not last:
                        ahead(t + 1, 0)
                    behind(t, b)

            ahead(0, 0)
            turn(0, False)
            with eng.Fori(1, NB // RG - 1) as t:
                turn(t, False)
            turn(NB // RG - 1, True)

        def rank_dve(dve, ch, key, C, K, NT, pos, tmap, S, kcol, parts=1, part_done=None):
            cnt, off, oh, sc, tmp, tcol = S["cnt"], S["off"], S["oh"], S["sc"], S["tmp"], S["tcol"]
            ti = S["ti"]
            with dve.Fori(0, K + 1) as k:
                ch.loop(k, 1)
                ch.link(dve.tensor_scalar(oh[:, 0:C], key, kcol[:, ds(k, 1)], None, ALU.is_equal, ALU.add,
                                          accum_out=cnt[:, ds(k, 1)]))
            ch.leave(K + 1)
            ch.link(dve.memset(tmp[:, 0:1], 0.0))
            dve.sem_inc(S["s_cnt"], 1)
            S["n_cnt"] += 1
            dve.wait_ge(S["s_tot"], S["n_cnt"] * 2 - 1)
            ch.link(dve.tensor_scalar(ti[:, 0:K], banks[0][:, 0:K], float(P - 1), None, ALU.add))
            ch.link(dve.tensor_scalar(ti[:, 0:K], ti[:, 0:K], 7, None, ALU.arith_shift_right))
            ch.link(dve.tensor_copy(tmp[:, 0:K], ti[:, 0:K]))
            ch.link(dve.tensor_tensor_scan(sc[:, 0:K], ones[:, 0:K], tmp[:, 0:K], 0.0, ALU.mult, ALU.add))
            ch.link(dve.tensor_tensor(tmp[:, 0:K], sc[:, 0:K], tmp[:, 0:K], ALU.subtract))
            ch.link(dve.tensor_scalar(off[:, 0:K], tmp[:, 0:K], float(P), -1.0, ALU.mult, ALU.add))
            ch.link(dve.memset(off[:, K:K + 1], float(NT * P - 1)))
            ch.link(dve.tensor_tensor(off[:, 0:K + 1], off[:, 0:K + 1], banks[1][:, 0:K + 1], ALU.add))
            ch.link(dve.tensor_scalar(ti[0:K, 0:1], banks[2][0:K, 0:1], float(P - 1), None, ALU.add))
            ch.link(dve.tensor_scalar(ti[0:K, 0:1], ti[0:K, 0:1], 7, None, ALU.arith_shift_right))
            dve.tensor_copy(tcol[0:K, :], ti[0:K, 0:1]).then_inc(S["s_tcol"], 1)
            CP = C // parts
            for part in range(parts):
                cols = key[:, part * CP:(part + 1) * CP]
                more = part < parts - 1
                ch.link(dve.memset(tmp[:, 0:CP], 0.0))
                with dve.Fori(0, K + 1) as k:
                    ch.loop(k, 4 + more)
                    ch.link(dve.tensor_scalar(oh[:, 0:CP], cols, kcol[:, ds(k, 1)], None, ALU.is_equal))
                    ch.link(dve.tensor_tensor_scan(sc[:, 0:CP], ones[:, 0:CP], oh[:, 0:CP], off[:, ds(k, 1)],
                                                   ALU.mult, ALU.add))
                    if more:
                        ch.link(dve.tensor_scalar(off[:, ds(k, 1)], sc[:, CP - 1:CP], 0.0, None, ALU.add))
                    ch.link(dve.tensor_tensor(oh[:, 0:CP], sc[:, 0:CP], oh[:, 0:CP], ALU.mult))
                    ch.link(dve.tensor_tensor(tmp[:, 0:CP], tmp[:, 0:CP], oh[:, 0:CP], ALU.add))
                ch.leave(K + 1)
                p = pos[:, part * CP:(part + 1) * CP]
                ch.link(dve.tensor_copy(p, tmp[:, 0:CP]))
                if part_done is not None:
                    part_done(p, CP)
            dve.wait_ge(S["s_tot"], S["n_cnt"] * 2)
            ch.link(dve.tensor_copy(tcol[0:K, :], banks[3][0:K, 0:1]))
            dve.tensor_scalar(oh[0:K, 0:NT], iota_row[0:K, 0:NT], tcol[0:K, :], None,
                              ALU.is_ge).then_inc(S["s_ge"], 1)
            dve.wait_ge(S["s_map"], S["n_cnt"])
            ch.link(dve.tensor_scalar(tmap[0:1, 0:NT], banks[4][0:1, 0:NT], float(K - 1), None, ALU.min))

        def rank_pe(pe, K, NT, S, n):
            cnt, tcol, oh = S["cnt"], S["tcol"], S["oh"]
            pe.wait_ge(S["s_cnt"], n)
            pe.matmul(banks[0][:, 0:K], ones[:, 0:P], cnt[:, 0:K], start=True, stop=True)
            pe.matmul(banks[1][:, 0:K + 1], tri_lt[:, :], cnt[:, 0:K + 1], start=True, stop=True)
            pe.matmul(banks[2][0:K, 0:1], cnt[:, 0:K], ones[:, 0:1], start=True, stop=True).then_inc(S["s_tot"], 1)
            pe.wait_ge(S["s_tcol"], n)
            pe.matmul(banks[3][0:K, 0:1], tri_le[0:K, 0:K], tcol[0:K, :], start=True, stop=True)\
                .then_inc(S["s_tot"], 1)
            pe.wait_ge(S["s_ge"], n)
            pe.matmul(banks[4][0:1, 0:NT], ones[0:K, 0:1], oh[0:K, 0:NT], start=True, stop=True)\
                .then_inc(S["s_map"], 1)

        def rank_scratch(ctx, tag, C, NT, region=None):
            n = max(C, NT)
            S = {}
            for i, name in enumerate(("oh", "sc", "tmp")):
                S[name] = region[:, i * n:(i + 1) * n] if region is not None else sb(ctx, f"{tag}_{name}", [P, n])
            S["cnt"], S["off"], S["tcol"] = (sb(ctx, f"{tag}_{k}", [P, w]) for k, w in
                                             (("cnt", 32), ("off", 32), ("tcol", 1)))
            S["ti"] = sb(ctx, f"{tag}_ti", [P, 32], i32)
            for k in ("s_cnt", "s_tot", "s_tcol", "s_ge", "s_map"):
                S[k] = new_sem(f"{tag}_{k}")
            S["n_cnt"] = 0
            return S

        def ln_stats_dve(dve, ch, act_sem, rt_sem, st6, n):
            rows_stats(dve, ch, resid, st6)
            dve.tensor_scalar(stats[:, :, 1], stats[:, :, 1], EPS, None, ALU.add).then_inc(act_sem, 1)
            dve.wait_ge(rt_sem, n)
            ch.link(dve.reciprocal(stats[:, :, 1], stats[:, :, 1]))

        def rows_stats(dve, ch, buf, st6):
            for t in range(NB):
                last = dve.bn_stats(st6[:, t, :], buf[:, t * D:(t + 1) * D])
            ch.link(last)
            for t in range(NB):
                last = dve.bn_aggr(stats[:, t, :], st6[:, t, :])
            ch.link(last)

        def ln_root_act(act, act_sem, rt_sem, n):
            act.wait_ge(act_sem, n)
            act.activation(stats[:, :, 1], stats[:, :, 1], ACT.Sqrt).then_inc(rt_sem, 1)

        def ln_rows_dve(dve, done):
            with dve.Fori(0, NB) as t:
                dve.tensor_scalar(rows(acc, t), rows(resid, t), stats[:, ds(t, 1), 0], stats[:, ds(t, 1), 1],
                                  ALU.subtract, ALU.mult).then_inc(done, 1)

        def table_view(table):
            return table.rearrange("(t p) d -> p t d", p=P)

        HALF = 8
        TURNS = EC // (2 * HALF)

        def scatter_ring(ctx, tag):
            return dict(idx=sb(ctx, f"{tag}_idx", [P, 2, HALF], i32), rec=sb(ctx, f"{tag}_rec", [P, 2, HALF, 4]),
                        full=new_sem(f"{tag}_full"),
                        sent=[new_sem(f"{tag}_sent{h}") for h in range(2)])

        def scatter_fill(eng, R, i, t, h, start=0):
            copy = eng.copy if i == 0 else eng.tensor_copy
            at_least(eng, R["sent"][h], t * 16 * HALF)
            c = (t + start) * 2 * HALF + h * HALF
            copy(R["idx"][:, h, :], (pos_src, pos_dst)[i][:, ds(c, HALF)]).then_inc(R["full"], 1)
            copy(R["rec"][:, h, :, :], rec[i][:, ds(c, HALF), :]).then_inc(R["full"], 1)

        def scatter_pool(pool, R, i, turns, by_dma=False):
            with pool.Fori(0, turns) as t:
                for h in range(2):
                    if by_dma:
                        pool.wait_ge(R["fill_landed"][h], t * 32 + 32)
                    else:
                        pool.wait_ge(R["full"], t * 4 + (2 * h + 2))
                    pool.nop(nofuse=True)
                    for j in range(HALF):
                        pool.indirect_dma_start(rec_dram[i][:, :], bass.IndirectOffsetOnAxis(R["idx"][:, h, j:j + 1], 0),
                                                R["rec"][:, h, j, :], None).then_inc(R["sent"][h], 16)
            for h in range(2):
                pool.wait_ge(R["sent"][h], turns * 16 * HALF)

        EARLY = 6

        def scatter_fill_sp(sp, R):
            def turn(t):
                for h in range(2):
                    at_least(sp, R["sent"][h], t * 16 * HALF)
                    c = t * 2 * HALF + h * HALF
                    sp.dma_start(R["idx"][:, h, :], pos_dst[:, ds(c, HALF)]).then_inc(R["fill_landed"][h], 16)
                    sp.dma_start(R["rec"][:, h, :, :], rec[1][:, ds(c, HALF), :]).then_inc(R["fill_landed"][h], 16)

            turn(0)
            with sp.Fori(1, EARLY) as t:
                turn(t)

        with phase() as ctx:
            sem = lambda n: new_sem(n)
            s_x, s_x2, s_e, s_iota, s_dve, s_edge, s_zero, s_fill, s_pad = (sem(n) for n in (
                "s_x", "s_x2", "s_e", "s_iota", "s_dve", "s_edge", "s_zero", "s_fill", "s_pad"))
            s_var, s_root, s_ln, s_tab = (sem(n) for n in ("s_var", "s_root", "s_ln", "s_tab"))
            ei = [sb(ctx, f"edge_i{i}", [P, EC], i32) for i in range(2)]
            ew = sb(ctx, "edge_w", [P, EC])
            S = rank_scratch(ctx, "edge", EC, ET, wbuf[:, 0:3 * ET])
            key = wbuf[:, 3 * ET:3 * ET + EC]
            tmpi = sb(ctx, "tmpi", [P, ET], i32)
            zeros = wbuf[:, 5 * ET:5 * ET + 2048]
            blank = wbuf[:, 5 * ET + 2048:5 * ET + 2048 + 4 * (ET + 1)]
            st6 = sb(ctx, "st6", [P, NB, 6])
            R = scatter_ring(ctx, "sort0")
            free = 14336
            q_of, r_of = wbuf[:, free:free + PCOL], wbuf[:, free + PCOL:free + 2 * PCOL]
            part = wbuf[:, free + 2 * PCOL:free + (2 + PARTS) * PCOL].rearrange("p (i c) -> p i c", i=PARTS)
            rest = wbuf[:, free + 8 * PCOL:free + 9 * PCOL]
            wb16 = wbuf[:, free + 9 * PCOL:free + 10 * PCOL].bitcast(bf16)[:, 0:PCOL]
            iota16 = wbuf[:, 16384:16384 + ET // 2].bitcast(f16)
            half = (P + PARTS * ET) // 2
            spread = [wbuf[:, 17000 + b * half:17000 + (b + 1) * half].bitcast(bf16) for b in range(2)]
            s_oneh, s_placed = new_sem("s_oneh"), new_sem("s_placed")
            s_sorted, s_blank = new_sem("s_sorted"), new_sem("s_blank")
            FILLS = len(rec_dram) + sum(-(-xs.shape[0] * D // P // 2048) for xs in xs_dram)
            block = ctx.enter_context(nc.Block())

            @block.sync
            def _(sp):
                sp.wait_ge(s_pad, 1)
                for buf, arr in ((ei[0], src), (ei[1], dst), (ew, edge_weight)):
                    sp.dma_start(buf[0:EFULL, :], arr[0:EFULL * EC].rearrange("(p c) -> p c", c=EC)).then_inc(s_e, 16)
                    sp.dma_start(buf[EFULL:P, 0:EREST],
                                 arr[EFULL * EC:EDGES].rearrange("(a c) -> a c", a=1)).then_inc(s_e, 16)
                sp.dma_start(resid[:, 0:(NB - 1) * D].rearrange("p (t d) -> p t d", d=D),
                             x[0:(NB - 1) * P, :].rearrange("(t p) d -> p t d", p=P)).then_inc(s_x, 16)
                sp.dma_start(resid[0:TAIL, (NB - 1) * D:], x[(NB - 1) * P:NODES, :]).then_inc(s_x2, 16)
                sp.wait_ge(s_zero, 2)
                for r in rec_dram:
                    sp.dma_start(r.rearrange("(p a) c -> p (a c)", p=P), blank).then_inc(s_fill, 16)
                for xs in xs_dram:
                    n = xs.shape[0] * D // P
                    v = xs.rearrange("(p a) d -> p (a d)", p=P)
                    for a in range(0, n, 2048):
                        sp.dma_start(v[:, a:min(a + 2048, n)], zeros[:, 0:min(2048, n - a)]).then_inc(s_fill, 16)
                sp.wait_ge(s_ln, NB)
                sp.dma_start(table_view(tab[0]), acc[:, 0:NB * D].rearrange("p (t d) -> p t d", d=D))\
                    .then_inc(s_tab, 16)
                sp.wait_ge(s_fill, 16 * FILLS)
                sp.wait_ge(s_tab, 16)

            @block.gpsimd
            def _(pool):
                pool.iota(tmpi[:, :], pattern=[[1, ET]], base=0, channel_multiplier=0).then_inc(s_iota, 1)
                pool.iota(S["ti"][:, 0:1], pattern=[[0, 1]], base=0, channel_multiplier=1).then_inc(s_iota, 1)
                pool.memset(blank, 0.0).then_inc(s_blank, 1)
                pool.memset(zeros, 0.0).then_inc(s_zero, 1)
                pool.wait_ge(s_blank, 1)
                pool.memset(blank.rearrange("p (a c) -> p a c", c=4)[:, :, 2], -1.0).then_inc(s_zero, 1)
                pool.wait_ge(s_fill, 16 * FILLS)
                scatter_pool(pool, R, 0, (EC - PCOL) // (2 * HALF))

            @block.scalar
            def _(act):
                act.wait_ge(s_sorted, 1)
                for h in range(2):
                    scatter_fill(act, R, 0, 0, h)
                with act.Fori(1, TURNS // 2) as t:
                    for h in range(2):
                        scatter_fill(act, R, 0, t, h)
                act.wait_ge(s_sorted, 2)
                ln_root_act(act, s_var, s_root, 1)
                with act.Fori(TURNS // 2, (EC - PCOL) // (2 * HALF)) as t:
                    for h in range(2):
                        scatter_fill(act, R, 0, t, h)

            @block.tensor
            def _(pe):
                rank_pe(pe, NB, ET, S, 1)
                rank_pe(pe, NB, ET, S, 2)

                def place(u, b, first=False, last=False):
                    pe.wait_ge(s_oneh, u * 2 + (b + 1))
                    for i in range(PARTS):
                        mm = pe.matmul(banks[i][:, 0:ET], spread[b][:, 0:P], spread[b][:, P + i * ET:P + (i + 1) * ET],
                                       start=first, stop=last, skip_group_check=True)
                    mm.then_inc(s_placed, 1)

                place(0, 0, first=True)
                place(0, 1)
                with pe.Fori(1, PCOL // 2 - 1) as u:
                    place(u, 0)
                    place(u, 1)
                place(PCOL // 2 - 1, 0)
                place(PCOL // 2 - 1, 1, last=True)

            @block.vector
            def _(dve):
                ch = Chain(dve, s_dve)
                dve.memset(ei[0][:, :], NB * P)
                dve.memset(ei[1][:, :], NB * P)
                dve.memset(ew[:, :], 0.0)
                ch.link(dve.memset(resid[:, (NB - 1) * D:], 0.0))
                dve.sem_inc(s_pad, 1)
                dve.memset(ones[:, :], 1.0)
                dve.wait_ge(s_iota, 2)
                dve.tensor_copy(iota_row[:, :], tmpi[:, :])
                ch.link(dve.tensor_copy(iota_col[:, :], S["ti"][:, 0:1]))
                dve.tensor_scalar(ident[:, :], iota_row[:, 0:P], iota_col[:, :], None, ALU.is_equal)
                dve.tensor_scalar(tri_lt[:, :], iota_row[:, 0:P], iota_col[:, :], None, ALU.is_gt)
                ch.link(dve.tensor_scalar(tri_le[:, :], iota_row[:, 0:P], iota_col[:, :], None, ALU.is_ge))
                dve.wait_ge(s_e, 16 * 6)
                for i in range(2):
                    to, frm = ei[i], ei[1 - i]
                    r = rec[i]
                    ch.link(dve.tensor_scalar(r[:, :, 0].bitcast(i32), frm[:, :], float(NODES - 1), None, ALU.min))
                    if i == 0:
                        dve.tensor_copy(r[:, :, 1], ew[:, :])
                    else:
                        dve.memset(r[:, :, 1], 1.0)
                    ch.link(dve.tensor_scalar(tmpi[:, 0:EC], to[:, :], 127, None, ALU.bitwise_and))
                    ch.link(dve.tensor_copy(r[:, :, 2], tmpi[:, 0:EC]))
                    dve.memset(r[:, :, 3], 0.0)
                    ch.link(dve.tensor_scalar(tmpi[:, 0:EC], to[:, :], 7, None, ALU.arith_shift_right))
                    ch.link(dve.tensor_copy(key, tmpi[:, 0:EC]))
                    pos = (pos_src, pos_dst)[i][:, 0:EC]

                    def dram_rows(p, n):
                        ch.link(dve.tensor_scalar(tmpi[:, 0:n], p, P - 1, None, ALU.bitwise_and))
                        ch.link(dve.tensor_scalar(p, p, 7, None, ALU.arith_shift_right))
                        if i == 0:
                            ch.link(dve.tensor_copy(r_of, tmpi[:, n - PCOL:n]))
                            ch.link(dve.tensor_copy(q_of, p[:, n - PCOL:n]))
                        ch.link(dve.scalar_tensor_tensor(p, tmpi[:, 0:n], float(ET + 1), p, ALU.mult, ALU.add))
                        dve.sem_inc(s_sorted, 1)

                    if i == 0:
                        mine = r[:, EC - PCOL:EC, :]
                        ch.link(dve.tensor_scalar(tmpi[:, 0:PCOL], mine[:, :, 0].bitcast(i32), 6, None,
                                                  ALU.arith_shift_right))
                        ch.link(dve.tensor_copy(part[:, 0, :], tmpi[:, 0:PCOL]))
                        ch.link(dve.tensor_scalar(tmpi[:, 0:PCOL], mine[:, :, 0].bitcast(i32), 63, None,
                                                  ALU.bitwise_and))
                        ch.link(dve.tensor_copy(part[:, 1, :], tmpi[:, 0:PCOL]))
                        ch.link(dve.tensor_scalar(part[:, 2, :], mine[:, :, 2], 1.0, None, ALU.add))
                        ch.link(dve.tensor_copy(rest, mine[:, :, 1]))
                        for k in range(3):
                            ch.link(dve.tensor_copy(wb16, rest))
                            ch.link(dve.tensor_copy(part[:, 3 + k, :], wb16))
                            ch.link(dve.tensor_tensor(rest, rest, part[:, 3 + k, :], ALU.subtract))
                        ch.link(dve.tensor_copy(iota16, iota_row[:, :]))

                    rank_dve(dve, ch, key, EC, NB, ET, pos, edge_map[i], S, iota_row,
                             parts=2 - i, part_done=dram_rows)
                dve.wait_ge(s_x, 16)
                dve.wait_ge(s_x2, 16)
                ln_stats_dve(dve, ch, s_var, s_root, st6, 1)
                ln_rows_dve(dve, s_ln)

                def one_hots(u, b):
                    at_least(dve, s_placed, (u - 1) * 2 + (b + 1))
                    n = ds(u * 2 + b, 1)
                    dve.tensor_scalar(spread[b][:, 0:P], iota16[:, 0:P], r_of[:, n], None, ALU.is_equal)
                    for i in range(PARTS):
                        last = dve.tensor_scalar(spread[b][:, P + i * ET:P + (i + 1) * ET], iota16, q_of[:, n],
                                                 part[:, i, n], ALU.is_equal, ALU.mult)
                    last.then_inc(s_oneh, 1)

                for b in range(2):
                    one_hots(0, b)
                with dve.Fori(1, PCOL // 2) as u:
                    for b in range(2):
                        one_hots(u, b)
                dve.wait_ge(s_placed, PCOL)

        def segment_sum(which, table, extra_sp):
            with phase() as ctx:
                tag = f"seg{which}_{table.name}"
                sem = lambda n: new_sem(f"{tag}_{n}")
                recs = sb(ctx, f"{tag}_recs", [P, ET, 4])
                hot = sb(ctx, f"{tag}_hot", [P, UN, P])
                idx = sb(ctx, f"{tag}_idx", [P, 2, 4], i32)
                wl = sb(ctx, f"{tag}_wl", [P, UN, 2])
                s_wl = sem("wl")
                G = sb(ctx, f"{tag}_G", [P, UN, AW])
                s_rec, s_zero, s_fld, s_hot, s_seg, s_acc = (sem(n) for n in (
                    "rec", "zero", "fld", "hot", "seg", "acc"))
                s_g = [sem(f"g{b}") for b in range(UN)]
                s_w, s_merge, s_ready = sem("w"), sem("merge"), sem("ready")
                ready = (s_ready, 1) if which == 0 else (s_rec, 16)
                block = ctx.enter_context(nc.Block())

                @block.sync
                def _(sp):
                    sp.dma_start(recs[:, :, :], rec_dram[which].rearrange("(p t) c -> p t c", p=P)[:, 0:ET, :])\
                        .then_inc(s_rec, 16)
                    extra_sp(sp, s_w, s_seg)

                @block.gpsimd
                def _(pool):
                    def turn(t):
                        for b in range(UN):
                            if b % 4 == 0:
                                pool.wait_ge(s_fld, t * 2 + (b // 4 + 1))
                            at_least(pool, s_seg, (t - 1) * UN + (b + 1))
                            pool.nop(nofuse=True)
                            pool.indirect_dma_start(G[:, b, 0:D], None, table[:, :],
                                                    bass.IndirectOffsetOnAxis(idx[:, b // 4, b % 4:b % 4 + 1], 0))\
                                .then_inc(s_g[b], 16)

                    turn(0)
                    with pool.Fori(1, ET // UN) as t:
                        turn(t)

                @block.vector
                def _(dve):
                    dve.memset(acc, 0.0).then_inc(s_zero, 1)
                    dve.memset(G[:, :, D:AW], 1.0).then_inc(s_zero, 1)
                    dve.wait_ge(s_zero, 2)
                    dve.wait_ge(s_rec, 16)
                    if which == 0:
                        ch = Chain(dve, s_merge)
                        sums = hot[:, :, :].rearrange("p b j -> p (b j)")[:, 0:ET]
                        row = recs[:, :, 0].bitcast(i32)
                        ch.link(dve.tensor_copy(sums, banks[1][:, 0:ET]))
                        ch.link(dve.scalar_tensor_tensor(sums, banks[0][:, 0:ET], 64.0, sums, ALU.mult, ALU.add))
                        ch.link(dve.tensor_tensor(row, row, sums, ALU.add))
                        for f, i in ((2, 2), (1, 3), (1, 4), (1, 5)):
                            ch.link(dve.tensor_tensor(recs[:, :, f], recs[:, :, f], banks[i][:, 0:ET], ALU.add))
                        dve.sem_inc(s_ready, 1)

                    def one_hot(t, b):
                        at_least(dve, s_seg, (t - 1) * UN + (b + 1))
                        if b % 4 == 0:
                            dve.wait_ge(s_wl, t * 2 + (b // 4 + 1))
                        dve.tensor_scalar(hot[:, b, :], iota_row[:, 0:P], wl[:, b, 1:2], wl[:, b, 0:1],
                                          ALU.is_equal, ALU.mult).then_inc(s_hot, 1)

                    def add(t, b, blk):
                        dve.wait_ge(s_seg, t * UN + (b + 1))
                        at_least(dve, s_acc, t * UN + b)
                        a = acc[:, ds(blk * AW, AW)]
                        dve.tensor_tensor(a, a, banks[b][:, 0:AW], ALU.add).then_inc(s_acc, 1)

                    def blocks(tile):
                        _, blks = nc.values_load_multi_w_load_instructions(
                            edge_map[which][0:1, ds(tile, UN // 2)], engines=(DVE,), min_val=0, max_val=NB - 1)
                        return blks

                    def turn(t, first=False):
                        if not first:
                            blks = blocks(t * UN - UN // 2)
                        for b in range(UN // 2):
                            one_hot(t, b)
                            if not first:
                                add(t - 1, b + UN // 2, blks[b])
                        blks = blocks(t * UN)
                        for b in range(UN // 2):
                            one_hot(t, b + UN // 2)
                            add(t, b, blks[b])

                    turn(0, True)
                    with dve.Fori(1, ET // UN) as t:
                        turn(t)
                    blks = blocks(ET - UN // 2)
                    for b in range(UN // 2):
                        add(ET // UN - 1, b + UN // 2, blks[b])

                @block.scalar
                def _(act):
                    act.wait_ge(*ready)

                    def turn(t):
                        for h in range(2):
                            for b in range(4 * h, 4 * h + 4):
                                at_least(act, s_g[b], t * 16)
                            r = recs[:, ds(t * UN + 4 * h, 4), :]
                            act.copy(idx[:, h, :], r[:, :, 0].bitcast(i32)).then_inc(s_fld, 1)
                            at_least(act, s_hot, (t - 1) * UN + (4 * h + 4))
                            act.copy(wl[:, 4 * h:4 * h + 4, :], r[:, :, 1:3]).then_inc(s_wl, 1)

                    turn(0)
                    with act.Fori(1, ET // UN) as t:
                        turn(t)

                @block.tensor
                def _(pe):
                    def turn(t):
                        for b in range(UN):
                            pe.wait_ge(s_g[b], t * 16 + 16)
                            pe.wait_ge(s_hot, t * UN + (b + 1))
                            at_least(pe, s_acc, (t - 1) * UN + (b + 1))
                            pe.matmul(banks[b][:, 0:AW], hot[:, b, :], G[:, b, :], start=True, stop=True)\
                                .then_inc(s_seg, 1)

                    pe.wait_ge(s_zero, 2)
                    pe.wait_ge(*ready)
                    turn(0)
                    with pe.Fori(1, ET // UN) as t:
                        turn(t)

        def load_experts(m, w, first, last):
            per = MOE[m]["PER"]

            def load(sp, sem, s_seg):
                for e in range(first, last):
                    sp.wait_ge(s_seg, (e + 1) * (ET // (last + 1)))
                    sp.dma_start(wbuf[:, e * per:(e + 1) * per], w[e, :, :]).then_inc(sem, 16)
                sp.wait_ge(sem, 16 * (last - first))
            return load

        HEAD = [ACC0 // m["PER"] for m in MOE]
        segment_sum(0, tab[0], load_experts(0, m1_w, 0, HEAD[0]))

        def moe_route(m, wg, bg, pre_dve, pre_pe, pre_act, pre_sp, pre_sems):
            E, NT = MOE[m]["E"], MOE[m]["NT"]
            with phase() as ctx:
                sem = lambda n: new_sem(f"rt{m}_{n}")
                s_dve, s_var, s_root, s_ln, s_in = (sem(n) for n in ("dve", "var", "root", "ln", "in"))
                s_tp, s_tc, s_gt, s_keep, s_ex, s_exd = (sem(n) for n in ("tp", "tc", "gt", "keep", "ex", "exd"))
                s_slot, s_row = (sem(n) for n in ("slot", "row"))
                stage = sb(ctx, f"rt{m}_stage", [P, RG, D])
                xT = sb(ctx, f"rt{m}_xT", [P, RG, 2 * P])
                S = rank_scratch(ctx, f"rt{m}", 2 * NB, NT)
                st6 = sb(ctx, f"rt{m}_st6", [P, NB, 6])
                wg_sb = sb(ctx, f"rt{m}_wg", [P, 2, E])
                bg_sb = sb(ctx, f"rt{m}_bg", [P, E])
                score = sb(ctx, f"rt{m}_score", [P, NB, E])
                top8 = sb(ctx, f"rt{m}_top8", [P, NB, 8])
                ind8 = sb(ctx, f"rt{m}_ind8", [P, NB, 8], mybir.dt.uint32)
                keyf = sb(ctx, f"rt{m}_key", [P, NB, 2])
                key2 = keyf[:, :, :].rearrange("p t s -> p (t s)")
                valid = sb(ctx, f"rt{m}_valid", [P, 2])
                pre = pre_sems(ctx)
                if m == 0:
                    R = scatter_ring(ctx, "early")
                    R["fill_landed"] = [sem(f"fill{h}") for h in range(2)]
                block = ctx.enter_context(nc.Block())

                @block.sync
                def _(sp):
                    sp.dma_start(wg_sb[:, :, :], wg).then_inc(s_in, 16)
                    sp.dma_start(bg_sb[:, :], bg.partition_broadcast(P)).then_inc(s_in, 16)
                    pre_sp(sp, pre)
                    if m == 0:
                        scatter_fill_sp(sp, R)
                    sp.wait_ge(s_in, 32)

                @block.scalar
                def _(act):
                    pre_act(act, pre, stage, xT)
                    ln_root_act(act, s_var, s_root, 1)

                    def keep(t, b):
                        act.wait_ge(s_ln, t * RG + (b + 1))
                        act.copy(rows(acc, t * RG + b), stage[:, b, :]).then_inc(s_keep, 1)

                    def columns(t, b):
                        act.wait_ge(s_tp, t * RG + (b + 1))
                        at_least(act, s_gt, (t - 1) * RG + (b + 1))
                        act.copy(xT[:, b, :], banks[b][:, 0:2 * P]).then_inc(s_tc, 1)

                    groups(act, keep, columns)
                    act.wait_ge(s_ex, 1)
                    act.activation(prob[:, 1, :], prob[:, 1, :], ACT.Exp).then_inc(s_exd, 1)

                @block.tensor
                def _(pe):
                    pre_pe(pe, pre, stage, xT)
                    pe.wait_ge(s_in, 32)

                    def turn_rows(t, b):
                        pe.wait_ge(s_ln, t * RG + (b + 1))
                        at_least(pe, s_tc, (t - 1) * RG + (b + 1))
                        for k in range(2):
                            mm = pe.transpose(banks[b][:, k * P:(k + 1) * P], stage[:, b, k * P:(k + 1) * P],
                                              ident[:, :])
                        mm.then_inc(s_tp, 1)

                    def gate(t, b):
                        pe.wait_ge(s_tc, t * RG + (b + 1))
                        for k in range(2):
                            mm = pe.matmul(banks[7][:, ds((t * RG + b) * E, E)], xT[:, b, k * P:(k + 1) * P],
                                           wg_sb[:, k, :], start=(k == 0), stop=(k == 1))
                        mm.then_inc(s_gt, 1)

                    groups(pe, turn_rows, gate)
                    rank_pe(pe, E, NT, S, 1)

                @block.vector
                def _(dve):
                    ch = Chain(dve, s_dve)
                    pre_dve(dve, ch, pre)
                    ln_stats_dve(dve, ch, s_var, s_root, st6, 1)

                    def turn(t):
                        for b in range(RG):
                            at_least(dve, s_tp, (t - 1) * RG + (b + 1))
                            at_least(dve, s_keep, (t - 1) * RG + (b + 1))
                            r = ds(t * RG + b, 1)
                            dve.tensor_scalar(stage[:, b, :], rows(resid, t * RG + b), stats[:, r, 0], stats[:, r, 1],
                                              ALU.subtract, ALU.mult).then_inc(s_ln, 1)

                    turn(0)
                    with dve.Fori(1, NB // RG) as t:
                        turn(t)
                    dve.wait_ge(s_in, 32)
                    dve.wait_ge(s_gt, NB)
                    ch.link(dve.tensor_tensor(score[:, :, :], banks[7][:, 0:NB * E].rearrange("p (t e) -> p t e", e=E),
                                              bg_sb[:, :].unsqueeze(1).to_broadcast([P, NB, E]), ALU.add))
                    for t in range(NB):
                        last = dve.max(top8[:, t, :], score[:, t, :])
                    ch.link(last)
                    for t in range(NB):
                        last = dve.max_index(ind8[:, t, :], top8[:, t, :], score[:, t, :])
                    ch.link(last)
                    dve.tensor_tensor(prob[:, 1, :], top8[:, :, 1], top8[:, :, 0], ALU.subtract).then_inc(s_ex, 1)
                    dve.wait_ge(s_exd, 1)
                    ch.link(dve.tensor_scalar(prob[:, 0, :], prob[:, 1, :], 1.0, None, ALU.add))
                    ch.link(dve.reciprocal(prob[:, 0, :], prob[:, 0, :]))
                    ch.link(dve.tensor_tensor(prob[:, 1, :], prob[:, 1, :], prob[:, 0, :], ALU.mult))
                    ch.link(dve.tensor_copy(keyf[:, :, :], ind8[:, :, 0:2]))
                    ch.link(dve.tensor_scalar(valid[:, 0:1], iota_col[:, :], float(TAIL), None, ALU.is_ge))
                    ch.link(dve.tensor_scalar(valid[:, 0:1], valid[:, 0:1], float(E), None, ALU.mult))
                    ch.link(dve.tensor_scalar(keyf[:, NB - 1, :], keyf[:, NB - 1, :], valid[:, 0:1], None, ALU.max))
                    rank_dve(dve, ch, key2, 2 * NB, E, NT, slot[:, :], exp_map[m], S, iota_row)
                    dve.sem_inc(s_slot, 1)

                @block.gpsimd
                def _(pool):
                    if m == 0:
                        scatter_pool(pool, R, 1, EARLY, by_dma=True)
                    pool.wait_ge(s_slot, 1)
                    pool.wait_ge(s_keep, NB)
                    for j in range(2 * NB):
                        pool.indirect_dma_start(xs_dram[m][:, :], bass.IndirectOffsetOnAxis(slot[:, j:j + 1], 0),
                                                acc[:, j // 2 * D:(j // 2 + 1) * D], None).then_inc(s_row, 16)
                    pool.wait_ge(s_row, 2 * NB * 16)

        def moe_experts(m, w, b1, b2, sort):
            E, H, NT, PER = (MOE[m][k] for k in ("E", "H", "NT", "PER"))
            NH, NJ = H // 512, H // P
            NG = NJ // 4
            hb, tb, yb, xb = banks[0:NH], banks[2:2 + NG], banks[4], banks[5]
            with phase() as ctx:
                sem = lambda n: new_sem(f"ff{m}_{n}")
                s_w, s_load, s_b1, s_b2, s_tx, s_xt, s_up, s_h, s_th, s_ht, s_dn, s_y = (sem(n) for n in (
                    "w", "load", "b1", "b2", "tx", "xt", "up", "h", "th", "ht", "dn", "y"))
                s_xs, s_st = ([sem(f"{n}{b}") for b in range(2)] for n in ("xs", "st"))
                xs = sb(ctx, f"ff{m}_xs", [P, 2, D])
                xT = sb(ctx, f"ff{m}_xT", [P, 2, P])
                h = sb(ctx, f"ff{m}_h", [P, H])
                hT = sb(ctx, f"ff{m}_hT", [P, NJ, P])
                y = sb(ctx, f"ff{m}_y", [P, 2, D])
                b1_sb = sb(ctx, f"ff{m}_b1", [P, E * NJ])
                b2_sb = sb(ctx, f"ff{m}_b2", [P, E * D])
                R = scatter_ring(ctx, "sort1") if sort else None
                block = ctx.enter_context(nc.Block())

                def pairs(eng, body):
                    body(0, sort)
                    n = TURNS - EARLY if sort else NT // 2
                    with eng.Fori(1, n) as u:
                        body(u, sort)
                    if n < NT // 2:
                        with eng.Fori(n, NT // 2) as u:
                            body(u, False)

                @block.sync
                def _(sp):
                    sp.dma_start(b1_sb[:, :], b1).then_inc(s_b1, 16)

                    def fetch(u, b):
                        at_least(sp, s_tx, u * 2 + (b - 1))
                        sp.dma_start(xs[:, b, :], xs_dram[m][ds((u * 2 + b) * P, P), :]).then_inc(s_xs[b], 16)

                    def store(u, b):
                        sp.wait_ge(s_y, u * 2 + (b + 1))
                        sp.dma_start(ys_dram[m][ds((u * 2 + b) * P, P), :], y[:, b, :]).then_inc(s_st[b], 16)

                    fetch(0, 0)
                    fetch(0, 1)
                    sp.dma_start(b2_sb[:, :], b2.partition_broadcast(P)).then_inc(s_b2, 16)

                    def body(u, sorting):
                        fetch(u + 1, 0)
                        if not isinstance(u, int):
                            store(u - 1, 1)
                        fetch(u + 1, 1)
                        store(u, 0)

                    pairs(sp, body)
                    store(NT // 2 - 1, 1)
                    for b in range(2):
                        sp.wait_ge(s_xs[b], 16 * (NT // 2 + 1))
                        sp.wait_ge(s_st[b], 16 * (NT // 2))

                @block.tensor
                def _(pe):
                    def turn_x(t, u, b):
                        pe.wait_ge(s_xs[b], u * 16 + 16)
                        at_least(pe, s_xt, t)
                        for k in range(2):
                            mm = pe.transpose(xb[:, k * P:(k + 1) * P], xs[:, b, k * P:(k + 1) * P], ident[:, :])
                        mm.then_inc(s_tx, 1)

                    def up(t, e):
                        pe.wait_ge(s_w, e + 1)
                        pe.wait_ge(s_xt, t + 1)
                        at_least(pe, s_h, t * NH)
                        for n in range(NH):
                            for k in range(2):
                                mm = pe.matmul(hb[n][:, :], xT[:, k, :],
                                               wbuf[:, ds(e * PER + (k * H + n * 512), 512)],
                                               start=(k == 0), stop=(k == 1))
                            mm.then_inc(s_up, 1)

                    def turn_h(t):
                        pe.wait_ge(s_h, t * NH + NH)
                        at_least(pe, s_ht, t * NG)
                        for g in range(NG):
                            for j in range(4):
                                mm = pe.transpose(tb[g][:, j * P:(j + 1) * P],
                                                  h[:, (4 * g + j) * P:(4 * g + j + 1) * P], ident[:, :])
                            mm.then_inc(s_th, 1)

                    def down(t, e):
                        pe.wait_ge(s_ht, t * NG + NG)
                        at_least(pe, s_y, t)
                        for j in range(NJ):
                            mm = pe.matmul(yb[:, 0:D], hT[:, j, :], wbuf[:, ds(e * PER + (2 * H + j * D), D)],
                                           start=(j == 0), stop=(j == NJ - 1))
                        mm.then_inc(s_dn, 1)

                    def expert(t):
                        return pe.value_load(exp_map[m][0:1, ds(t, 1)], min_val=0, max_val=E - 1)

                    turn_x(0, 0, 0)

                    def body(u, sorting):
                        for b in range(2):
                            t = u * 2 + b
                            up(t, expert(t))
                            turn_x(t + 1, u + b, 1 - b)
                            if not (isinstance(t, int) and t == 0):
                                down(t - 1, expert(t - 1))
                            turn_h(t)

                    pairs(pe, body)
                    down(NT - 1, expert(NT - 1))

                @block.scalar
                def _(act):
                    act.wait_ge(s_b1, 16)

                    def turn(t):
                        e = act.value_load(exp_map[m][0:1, ds(t, 1)], min_val=0, max_val=E - 1)
                        for g in range(NG):
                            act.wait_ge(s_th, t * NG + (g + 1))
                            at_least(act, s_dn, t)
                            for j in range(4):
                                q = 4 * g + j
                                last = act.activation(hT[:, q, :], tb[g][:, j * P:(j + 1) * P], ACT.Relu,
                                                      bias=b1_sb[:, ds(e * NJ + q, 1)])
                            last.then_inc(s_ht, 1)

                    turn(0)
                    with act.Fori(1, NT) as t:
                        turn(t)

                @block.vector
                def _(dve):
                    def copy_x(t):
                        dve.wait_ge(s_tx, t + 1)
                        at_least(dve, s_up, t * NH)
                        dve.tensor_copy(xT[:, :, :].rearrange("p k n -> p (k n)"), xb[:, 0:2 * P]).then_inc(s_xt, 1)

                    def copy_h(t):
                        at_least(dve, s_th, t * NG)
                        for n in range(NH):
                            dve.wait_ge(s_up, t * NH + (n + 1))
                            dve.tensor_copy(h[:, n * 512:(n + 1) * 512], hb[n][:, :]).then_inc(s_h, 1)

                    def copy_y(t, u, b):
                        e = dve.value_load(exp_map[m][0:1, ds(t, 1)], min_val=0, max_val=E - 1)
                        if isinstance(t, int):
                            dve.wait_ge(s_b2, 16)
                        dve.wait_ge(s_dn, t + 1)
                        at_least(dve, s_st[b], u * 16)
                        dve.tensor_tensor(y[:, b, :], yb[:, 0:D], b2_sb[:, ds(e * D, D)], ALU.add).then_inc(s_y, 1)

                    copy_x(0)

                    def body(u, sorting):
                        for b in range(2):
                            t = u * 2 + b
                            copy_h(t)
                            copy_x(t + 1)
                            if not (isinstance(t, int) and t == 0):
                                copy_y(t - 1, u - 1 + b, 1 - b)
                            if sorting:
                                scatter_fill(dve, R, 1, u, b, EARLY)

                    pairs(dve, body)
                    copy_y(NT - 1, NT // 2 - 1, 1)

                @block.gpsimd
                def _(pool):
                    pool.sem_inc(s_w, HEAD[m])
                    for e in range(HEAD[m], E):
                        pool.dma_start(wbuf[:, e * PER:(e + 1) * PER], w[e, :, :]).then_inc(s_load, 16)
                        pool.wait_ge(s_load, 16 * (e - HEAD[m] + 1))
                        pool.sem_inc(s_w, 1)
                    if sort:
                        scatter_pool(pool, R, 1, TURNS - EARLY)

        def moe_combine(m, post_dve, post_act, post_sp, post_sems):
            target = resid if m == 0 else acc
            with phase() as ctx:
                sem = lambda n: new_sem(f"cb{m}_{n}")
                s_idx, s_use, s_add, s_dve, s_pre = (sem(n) for n in ("idx", "use", "add", "dve", "pre"))
                s_g = [sem(f"g{j}") for j in range(2 * RG)]
                Y = sb(ctx, f"cb{m}_Y", [P, 2 * RG, D])
                idx = sb(ctx, f"cb{m}_idx", [P, 2 * NB], i32)
                post = post_sems(ctx)
                beta_sb = post.get("B")
                st6 = sb(ctx, f"cb{m}_st6", [P, RG, 6])
                agg = sb(ctx, f"cb{m}_agg", [P, RG, 2])
                s_bn, s_agg, s_cp = (sem(n) for n in ("bn", "agg", "cp"))
                block = ctx.enter_context(nc.Block())

                @block.gpsimd
                def _(pool):
                    for j in range(2 * NB):
                        b = j % (2 * RG)
                        if j >= 2 * RG:
                            pool.wait_ge(s_add, j - 2 * RG + 1)
                        if j == 0:
                            pool.wait_ge(s_idx, 1)
                        pool.indirect_dma_start(Y[:, b, :], None, ys_dram[m][:, :],
                                                bass.IndirectOffsetOnAxis(idx[:, j:j + 1], 0)).then_inc(s_g[b], 16)

                @block.vector
                def _(dve):
                    ch = Chain(dve, s_dve)
                    dve.tensor_scalar(idx[:, :], slot[:, :], float(MOE[m]["NT"] * P - 1), None, ALU.min)\
                        .then_inc(s_idx, 1)
                    if m == 1:
                        ln_rows_dve(dve, s_pre)
                        dve.wait_ge(s_pre, NB)

                    def turn(t):
                        for j in range(2 * RG):
                            b, n = j // 2, t * RG + j // 2
                            dve.wait_ge(s_g[j], t * 16 + 16)
                            r = target[:, ds(n * D, D)]
                            if j % 2:
                                dve.wait_ge(s_add, t * 2 * RG + j)
                            dve.scalar_tensor_tensor(r, Y[:, j, :], prob[:, j % 2, ds(n, 1)], r,
                                                     ALU.mult, ALU.add).then_inc(s_add, 1)
                            if j % 2:
                                dve.wait_ge(s_add, t * 2 * RG + (j + 1))
                                at_least(dve, s_agg, (t - 1) * RG + (b + 1))
                                dve.nop(nofuse=True)
                                dve.bn_stats(st6[:, b, :], r).then_inc(s_bn, 1)
                                if beta_sb is not None:
                                    dve.tensor_tensor(rows(resid, n), rows(resid, n), beta_sb[:, :], ALU.add)\
                                        .then_inc(post["beta"], 1)
                        at_least(dve, s_cp, t)
                        for b in range(RG):
                            dve.wait_ge(s_bn, t * RG + (b + 1))
                            dve.nop(nofuse=True)
                            dve.bn_aggr(agg[:, b, :], st6[:, b, :]).then_inc(s_agg, 1)
                        dve.wait_ge(s_agg, t * RG + RG)
                        dve.tensor_copy(stats[:, ds(t * RG, RG), :], agg[:, :, :]).then_inc(s_cp, 1)

                    if m == 1:
                        dve.wait_ge(post["w"], 32)
                    turn(0)
                    with dve.Fori(1, NB // RG) as t:
                        turn(t)
                    dve.wait_ge(s_cp, NB // RG)
                    dve.tensor_scalar(stats[:, :, 1], stats[:, :, 1], EPS, None, ALU.add).then_inc(post["var"], 1)
                    dve.wait_ge(post["root"], 1)
                    ch.link(dve.reciprocal(stats[:, :, 1], stats[:, :, 1]))
                    post_dve(dve, ch, post)

                @block.scalar
                def _(act):
                    post_act(act, post)

                @block.sync
                def _(sp):
                    post_sp(sp, post)

        def pre0_sems(ctx):
            p = {k: new_sem(f"l0_{k}") for k in ("w", "st", "tp", "tc", "mm", "up", "bias")}
            p["W"] = sb(ctx, "l0_W", [P, 2, D])
            p["B"] = sb(ctx, "l0_B", [P, D])
            return p

        def pre0_sp(sp, p):
            sp.dma_start(p["W"][:, :, :], l0_w).then_inc(p["w"], 16)
            sp.dma_start(p["B"][:, :], l0_b.partition_broadcast(P)).then_inc(p["w"], 16)

        def pre0_act(act, p, stage, xT):
            def sums(t, b):
                at_least(act, p["tp"], (t - 1) * RG + (b + 1))
                act.copy(stage[:, b, :], acc[:, ds((t * RG + b) * AW, D)]).then_inc(p["st"], 1)

            def columns(t, b):
                act.wait_ge(p["tp"], t * RG + (b + 1))
                at_least(act, p["mm"], (t - 1) * RG + (b + 1))
                act.copy(xT[:, b, :], banks[b][:, 0:2 * P]).then_inc(p["tc"], 1)

            groups(act, sums, columns)
            act.wait_ge(p["mm"], NB)

        def pre0_pe(pe, p, stage, xT):
            pe.wait_ge(p["w"], 32)

            def turn_rows(t, b):
                pe.wait_ge(p["st"], t * RG + (b + 1))
                at_least(pe, p["tc"], (t - 1) * RG + (b + 1))
                for k in range(2):
                    mm = pe.transpose(banks[b][:, k * P:(k + 1) * P], stage[:, b, k * P:(k + 1) * P], ident[:, :])
                mm.then_inc(p["tp"], 1)

            def linear(t, b):
                pe.wait_ge(p["tc"], t * RG + (b + 1))
                at_least(pe, p["up"], t * RG + (b - (b > 0)))
                for k in range(2):
                    mm = pe.matmul(banks[5 + b % 2][:, 0:D], xT[:, b, k * P:(k + 1) * P], p["W"][:, k, :],
                                   start=(k == 0), stop=(k == 1))
                mm.then_inc(p["mm"], 1)

            groups(pe, turn_rows, linear)

        def pre0_dve(dve, ch, p):
            dve.wait_ge(p["w"], 32)

            def bias(t, b):
                r = rows(resid, t * RG + b)
                dve.tensor_tensor(r, r, p["B"][:, :], ALU.add).then_inc(p["bias"], 1)

            def add(t, b):
                dve.wait_ge(p["mm"], t * RG + (b + 1))
                dve.wait_ge(p["bias"], t * RG + (b + 1))
                r = rows(resid, t * RG + b)
                dve.tensor_tensor(r, r, banks[5 + b % 2][:, 0:D], ALU.add).then_inc(p["up"], 1)

            groups(dve, bias, add)
            dve.wait_ge(p["up"], NB)

        moe_route(0, m1_wg, m1_bg, pre0_dve, pre0_pe, pre0_act, pre0_sp, pre0_sems)

        moe_experts(0, m1_w, m1_b1, m1_b2, True)

        def post0_sems(ctx):
            p = {k: new_sem(f"post0_{k}") for k in ("var", "root", "ln", "tab")}
            return p

        def post0_dve(dve, ch, p):
            ln_rows_dve(dve, p["ln"])

        def post0_act(act, p):
            ln_root_act(act, p["var"], p["root"], 1)

        def post0_sp(sp, p):
            sp.wait_ge(p["ln"], NB)
            sp.dma_start(table_view(tab[1]), acc[:, 0:NB * D].rearrange("p (t d) -> p t d", d=D)).then_inc(p["tab"], 16)
            sp.wait_ge(p["tab"], 16)

        moe_combine(0, post0_dve, post0_act, post0_sp, post0_sems)

        SAGE_AT = (HEAD[1] - 2) * MOE[1]["PER"]
        W1 = wbuf[:, SAGE_AT:SAGE_AT + 4 * HID].rearrange("p (q n) -> p q n", q=4)
        W2 = wbuf[:, SAGE_AT + 4 * HID:SAGE_AT + 4 * HID + 8 * D].rearrange("p (q n) -> p q n", q=4)
        experts_early = load_experts(1, m2_w, 0, HEAD[1] - 2)

        def load_phase7(sp, sem, s_seg):
            for to, w in ((W1[:, 0:2, :], g_w1l), (W1[:, 2:4, :], g_w1r), (W2, g_w2)):
                sp.dma_start(to, w).then_inc(s_sage, 16)
            experts_early(sp, sem, s_seg)
            sp.wait_ge(s_sage, 48)

        s_sage = nc.alloc_semaphore("s_sage")
        segment_sum(1, tab[1], load_phase7)

        with phase() as ctx:
            sem = lambda n: new_sem(f"sage_{n}")
            s_w, s_dve, s_in, s_tp, s_tc, s_m1, s_h, s_th, s_ht, s_m2, s_z, s_st = (sem(n) for n in (
                "w", "dve", "in", "tp", "tc", "m1", "h", "th", "ht", "m2", "z", "st"))
            B1 = sb(ctx, "sage_B1", [P, HID])
            B2 = sb(ctx, "sage_B2", [P, D])
            mx = sb(ctx, "sage_mx", [P, 2, D])
            mxT = sb(ctx, "sage_mxT", [P, 4, P])
            h = sb(ctx, "sage_h", [P, HID])
            hT = sb(ctx, "sage_hT", [P, 4, P])
            z = sb(ctx, "sage_z", [P, D])
            accv = acc.rearrange("p (t a) -> p t a", a=AW)
            block = ctx.enter_context(nc.Block())

            @block.sync
            def _(sp):
                sp.dma_start(B1[:, :], g_b1l.partition_broadcast(P)).then_inc(s_w, 16)
                sp.dma_start(B2[:, :], g_b2l.partition_broadcast(P)).then_inc(s_w, 16)
                with sp.Fori(0, NB) as t:
                    sp.wait_ge(s_z, t * 2 + 1)
                    sp.dma_start(tab[2][ds(t * P, P), :], z[:, :]).then_inc(s_st, 16)
                sp.wait_ge(s_st, NB * 16)

            @block.tensor
            def _(pe):

                def turn_rows(t):
                    pe.wait_ge(s_in, t * 2 + 2)
                    at_least(pe, s_tc, t)
                    for q in range(4):
                        mm = pe.transpose(banks[0][:, q * P:(q + 1) * P],
                                          mx[:, q // 2, (q % 2) * P:(q % 2 + 1) * P], ident[:, :])
                    mm.then_inc(s_tp, 1)

                def first_layer(t):
                    pe.wait_ge(s_tc, t + 1)
                    at_least(pe, s_h, t)
                    for q in range(4):
                        mm = pe.matmul(banks[1][:, :], mxT[:, q, :], W1[:, q, :], start=(q == 0), stop=(q == 3))
                    mm.then_inc(s_m1, 1)

                def turn_hidden(t):
                    pe.wait_ge(s_h, t + 1)
                    at_least(pe, s_ht, t)
                    for q in range(4):
                        mm = pe.transpose(banks[2][:, q * P:(q + 1) * P], h[:, q * P:(q + 1) * P], ident[:, :])
                    mm.then_inc(s_th, 1)

                def second_layer(t):
                    pe.wait_ge(s_ht, t + 1)
                    at_least(pe, s_z, t * 2)
                    for q in range(4):
                        mm = pe.matmul(banks[3][:, :], hT[:, q, :], W2[:, q, :], start=(q == 0), stop=(q == 3))
                    mm.then_inc(s_m2, 1)

                turn_rows(0)
                first_layer(0)
                turn_rows(1)
                turn_hidden(0)
                with pe.Fori(1, NB - 1) as t:
                    first_layer(t)
                    turn_rows(t + 1)
                    second_layer(t - 1)
                    turn_hidden(t)
                first_layer(NB - 1)
                second_layer(NB - 2)
                turn_hidden(NB - 1)
                second_layer(NB - 1)

            @block.scalar
            def _(act):
                def copy_rows(t):
                    act.wait_ge(s_tp, t + 1)
                    at_least(act, s_m1, t)
                    act.activation(mxT[:, :, :].rearrange("p k n -> p (k n)"), banks[0][:, :], ACT.Copy).then_inc(s_tc, 1)

                def relu(t):
                    act.wait_ge(s_th, t + 1)
                    at_least(act, s_m2, t)
                    act.activation(hT[:, :, :].rearrange("p k n -> p (k n)"), banks[2][:, :], ACT.Relu).then_inc(s_ht, 1)

                copy_rows(0)
                copy_rows(1)
                relu(0)
                with act.Fori(1, NB - 1) as t:
                    copy_rows(t + 1)
                    relu(t)
                relu(NB - 1)

            @block.vector
            def _(dve):
                ch = Chain(dve, s_dve)
                dve.wait_ge(s_w, 32)
                ch.link(dve.tensor_scalar(inv_cnt[:, :], accv[:, :, D], 1.0, None, ALU.max))
                ch.link(dve.reciprocal(inv_cnt[:, :], inv_cnt[:, :]))

                def rows_in(t):
                    at_least(dve, s_tp, t)
                    dve.tensor_scalar(mx[:, 0, :], acc[:, ds(t * AW, D)], inv_cnt[:, ds(t, 1)], None, ALU.mult)\
                        .then_inc(s_in, 1)
                    dve.tensor_scalar(mx[:, 1, :], rows(resid, t), stats[:, ds(t, 1), 0], stats[:, ds(t, 1), 1],
                                      ALU.subtract, ALU.mult).then_inc(s_in, 1)

                def hidden(t):
                    dve.wait_ge(s_m1, t + 1)
                    at_least(dve, s_th, t)
                    dve.tensor_tensor(h[:, :], banks[1][:, :], B1[:, :], ALU.add).then_inc(s_h, 1)

                def results(t):
                    ch.link(dve.tensor_tensor(rows(resid, t), rows(resid, t), B2[:, :], ALU.add))
                    dve.wait_ge(s_m2, t + 1)
                    at_least(dve, s_st, t * 16)
                    dve.tensor_copy(z[:, :], banks[3][:, 0:D]).then_inc(s_z, 1)
                    dve.tensor_tensor(rows(resid, t), rows(resid, t), banks[3][:, D:2 * D], ALU.add).then_inc(s_z, 1)

                rows_in(0)
                rows_in(1)
                hidden(0)
                dve.wait_ge(s_in, 4)
                with dve.Fori(1, NB - 1) as t:
                    ch.loop(t - 1, 1)
                    rows_in(t + 1)
                    hidden(t)
                    results(t - 1)
                ch.leave(NB - 2)
                hidden(NB - 1)
                results(NB - 2)
                dve.wait_ge(s_in, 2 * NB)
                results(NB - 1)

        segment_sum(1, tab[2], load_experts(1, m2_w, HEAD[1] - 2, HEAD[1]))

        def pre1_sems(ctx):
            return dict(up=new_sem("pre1_up"))

        def pre1_dve(dve, ch, p):
            with dve.Fori(0, NB) as t:
                dve.scalar_tensor_tensor(rows(resid, t), acc[:, ds(t * AW, D)], inv_cnt[:, ds(t, 1)],
                                         rows(resid, t), ALU.mult, ALU.add).then_inc(p["up"], 1)
            dve.wait_ge(p["up"], NB)

        moe_route(1, m2_wg, m2_bg, pre1_dve, lambda *a: None, lambda *a: None, lambda sp, p: None, pre1_sems)

        moe_experts(1, m2_w, m2_b1, m2_b2, False)

        def post1_sems(ctx):
            p = {k: new_sem(f"post1_{k}") for k in ("w", "var", "root", "scaled", "up", "out", "beta")}
            p["G"] = sb(ctx, "post1_G", [P, D])
            p["B"] = sb(ctx, "post1_B", [P, D])
            return p

        def post1_dve(dve, ch, p):
            def scale(t, b):
                n = t * RG + b
                dve.scalar_tensor_tensor(rows(acc, n), rows(acc, n), stats[:, ds(n, 1), 0], p["G"][:, :],
                                         ALU.subtract, ALU.mult).then_inc(p["scaled"], 1)

            def finish(t, b):
                n = t * RG + b
                dve.wait_ge(p["scaled"], n + 1)
                dve.scalar_tensor_tensor(rows(resid, n), rows(acc, n), stats[:, ds(n, 1), 1], rows(resid, n),
                                         ALU.mult, ALU.add).then_inc(p["up"], 1)

            dve.wait_ge(p["beta"], NB)
            groups(dve, scale, finish)

        def post1_act(act, p):
            ln_root_act(act, p["var"], p["root"], 1)

        def post1_sp(sp, p):
            sp.dma_start(p["G"][:, :], gamma.partition_broadcast(P)).then_inc(p["w"], 16)
            sp.dma_start(p["B"][:, :], beta.partition_broadcast(P)).then_inc(p["w"], 16)
            with sp.Fori(0, NB - 1) as t:
                sp.wait_ge(p["up"], t + 1)
                sp.dma_start(out[ds(t * P, P), :], rows(resid, t)).then_inc(p["out"], 16)
            sp.wait_ge(p["up"], NB)
            sp.dma_start(out[(NB - 1) * P:NODES, :], resid[0:TAIL, (NB - 1) * D:]).then_inc(p["out"], 16)
            sp.wait_ge(p["out"], NB * 16)

        moe_combine(1, post1_dve, post1_act, post1_sp, post1_sems)


def kernel(**inputs):
    import numpy as _np
    import concourse.bacc as _bacc
    from concourse import mybir as _mybir
    from concourse.bass_utils import run_bass_kernel_spmd as _run

    def up(a, *order):
        a = _np.transpose(_np.asarray(a), order) if order else _np.asarray(a)
        return a.reshape(a.shape[0] // 128, 128, -1).transpose(1, 0, 2)

    def experts(w_up, w_down):
        parts = [w.reshape(w.shape[0], w.shape[1] // 128, 128, -1).transpose(0, 2, 1, 3).reshape(w.shape[0], 128, -1)
                 for w in (w_up, w_down)]
        return _np.concatenate(parts, axis=2)

    g = {k: _np.asarray(v) for k, v in inputs.items()}
    args = dict(
        x=g["x"], src=g["src"], dst=g["dst"], edge_weight=g["edge_weight"],
        l0_w=up(g["L0_gnn_W"], 1, 0), l0_b=g["L0_gnn_b"],
        m1_wg=up(g["L0_ffn_Wg"], 1, 0), m1_bg=g["L0_ffn_bg"],
        m1_w=experts(g["L0_ffn_W1"].transpose(0, 2, 1), g["L0_ffn_W2"].transpose(0, 2, 1)),
        m1_b1=g["L0_ffn_b1"].reshape(8 * 8, 128).T, m1_b2=g["L0_ffn_b2"].reshape(-1),
        g_w1l=up(g["L1_gnn_W1l"], 1, 0), g_b1l=g["L1_gnn_b1l"], g_w1r=up(g["L1_gnn_W1r"], 1, 0),
        g_w2=_np.concatenate([up(g["L1_gnn_W2l"], 1, 0), up(g["L1_gnn_W2r"], 1, 0)], axis=2),
        g_b2l=g["L1_gnn_b2l"],
        m2_wg=up(g["L1_ffn_gate_w"]), m2_bg=g["L1_ffn_gate_b"], m2_w=experts(g["L1_ffn_w1"], g["L1_ffn_w2"]),
        m2_b1=g["L1_ffn_b1"].reshape(16 * 4, 128).T, m2_b2=g["L1_ffn_b2"].reshape(-1),
        gamma=g["L1_ffn_gamma"], beta=g["L1_ffn_beta"])
    nc = _bacc.Bacc("TRN2", target_bir_lowering=False, num_devices=1)
    arrays, aps = {}, {}
    for name, a in args.items():
        a = _np.ascontiguousarray(a)
        arrays[f"in_{name}"] = a
        aps[name] = nc.dram_tensor(f"in_{name}", a.shape, _mybir.dt.from_np(a.dtype), kind="ExternalInput").ap()
    aps["out"] = nc.dram_tensor("out_0", (3125, 256), _mybir.dt.float32, kind="ExternalOutput").ap()
    gnn_moe_program(nc, **aps)
    r = _run(nc, [arrays], core_ids=[0])
    return r.results[0]["out_0"]
```
